# Optimizing a Trainium2 kernel written in Bass

```python
import numpy as np
import jax
import jax.numpy as jnp

def _softmax(x, axis=-1):
    return jax.nn.softmax(x, axis=axis)

def _gelu(x):
    return jax.nn.gelu(x, approximate=True)

def _silu(x):
    return jax.nn.silu(x)

def _sigmoid(x):
    return jax.nn.sigmoid(x)

def _layernorm(x, axis=-1, eps=1e-05):
    m = jnp.mean(x, axis=axis, keepdims=True)
    v = jnp.var(x, axis=axis, keepdims=True)
    return (x - m) / jnp.sqrt(v + eps)

def _scatter_add(tgt, idx, src, axis=0):
    return tgt.at[idx].add(src)

def _segment_sum(src, seg, n):
    return jax.ops.segment_sum(src, seg, n)
kernel_name = 'mk_conv_attn_hybrid_d2_conv_nhwc256_r2_813df9'

def setup_inputs(seed: int=0):
    np.random.seed(seed)
    _w = jnp.asarray

    def _rec_inputs():
        import jax
        import jax.numpy as jnp
        _gk = jax.random.key(seed)
        x = -0.0005207 + 1.001 * jax.random.normal(jax.random.fold_in(_gk, 1), (2, 32, 32, 128), jnp.float32)
        return x
    x = _rec_inputs()

    def _L0_conv_setup():
        import jax, jax.numpy as jnp
        import numpy as np
        DIM, K, NH = (128, 7, 8)

        def _nbhd_idx(n, k):
            start = jnp.clip(jnp.arange(n) - k // 2, 0, n - k)
            idx = start[:, None] + jnp.arange(k)[None, :]
            bias = idx - jnp.arange(n)[:, None] + (k - 1)
            return (idx, bias)
        key = jax.random.key(seed)
        ks = jax.random.split(key, 8)
        s = lambda k_, sh, fan: jax.random.normal(k_, sh, jnp.float32) * fan ** (-0.5)
        return {'x': jax.random.normal(ks[0], (2, 32, 32, DIM), jnp.float32), 'qkv_w': s(ks[1], (DIM, 3 * DIM), DIM), 'qkv_b': jnp.zeros((3 * DIM,), jnp.float32), 'rpb': 0.02 * jax.random.normal(ks[2], (NH, 2 * K - 1, 2 * K - 1), jnp.float32), 'proj_w': s(ks[3], (DIM, DIM), DIM), 'proj_b': jnp.zeros((DIM,), jnp.float32), 'g1_w': s(ks[4], (DIM, DIM // 4), DIM), 'g1_b': jnp.zeros((DIM // 4,), jnp.float32), 'g2_w': s(ks[5], (DIM // 4, 1), DIM // 4), 'g2_b': jnp.zeros((1,), jnp.float32), 'ln_g': jnp.ones((DIM,), jnp.float32), 'ln_b': jnp.zeros((DIM,), jnp.float32)}
    _L0_conv_all = _L0_conv_setup()
    _L0_conv_in = {k: v for k, v in _L0_conv_all.items() if k in ('qkv_w', 'qkv_b', 'rpb', 'proj_w', 'proj_b', 'g1_w', 'g1_b', 'g2_w', 'g2_b', 'ln_g', 'ln_b')}
    del _L0_conv_all

    def _L1_attn_setup():
        import jax, jax.numpy as jnp
        import numpy as np
        B, L, D, U = (4, 512, 128, 32)
        key = jax.random.key(seed)
        k1, k2, k3, k4 = jax.random.split(key, 4)
        return {'inputs': jax.random.normal(k1, (B, L, D), dtype=jnp.float32), 'Wt': jax.random.normal(k2, (D, U), dtype=jnp.float32) * (1.0 / np.sqrt(D)), 'Wx': jax.random.normal(k3, (D, U), dtype=jnp.float32) * (1.0 / np.sqrt(D)), 'bh': jnp.zeros((U,), dtype=jnp.float32), 'Wa': jax.random.normal(k4, (U, 1), dtype=jnp.float32) * (1.0 / np.sqrt(U)), 'ba': jnp.zeros((1,), dtype=jnp.float32)}
    _L1_attn_all = _L1_attn_setup()
    _L1_attn_in = {k: v for k, v in _L1_attn_all.items() if k in ('Wt', 'Wx', 'bh', 'Wa', 'ba')}
    del _L1_attn_all

    def _L1_ffn_setup():
        import math
        import jax, jax.numpy as jnp
        import numpy as np
        CAPACITY_FACTOR = 1.25
        key = jax.random.key(seed)
        ks = jax.random.split(key, 5)
        B, L, D, F, E = (8, 4096, 128, 512, 8)
        h = jax.random.normal(ks[0], (B, L, D), dtype=jnp.float32)
        gate_w = jax.random.normal(ks[1], (D, E), dtype=jnp.float32) * 0.02
        gate_b = jnp.zeros((E,), dtype=jnp.float32)
        w1 = jax.random.normal(ks[2], (E, D, F), dtype=jnp.float32) * (1.0 / math.sqrt(D))
        b1 = jnp.zeros((E, F), dtype=jnp.float32)
        w2 = jax.random.normal(ks[3], (E, F, D), dtype=jnp.float32) * (1.0 / math.sqrt(F))
        b2 = jnp.zeros((E, D), dtype=jnp.float32)
        return {'h': h, 'gate_w': gate_w, 'gate_b': gate_b, 'w1': w1, 'b1': b1, 'w2': w2, 'b2': b2}
    _L1_ffn_all = _L1_ffn_setup()
    _L1_ffn_in = {k: v for k, v in _L1_ffn_all.items() if k in ('gate_w', 'gate_b', 'w1', 'b1', 'w2', 'b2')}
    del _L1_ffn_all
    return {'x': x, 'L0_conv_qkv_w': _L0_conv_in['qkv_w'], 'L0_conv_qkv_b': _L0_conv_in['qkv_b'], 'L0_conv_rpb': _L0_conv_in['rpb'], 'L0_conv_proj_w': _L0_conv_in['proj_w'], 'L0_conv_proj_b': _L0_conv_in['proj_b'], 'L0_conv_g1_w': _L0_conv_in['g1_w'], 'L0_conv_g1_b': _L0_conv_in['g1_b'], 'L0_conv_g2_w': _L0_conv_in['g2_w'], 'L0_conv_g2_b': _L0_conv_in['g2_b'], 'L0_conv_ln_g': _L0_conv_in['ln_g'], 'L0_conv_ln_b': _L0_conv_in['ln_b'], 'L1_attn_Wt': _L1_attn_in['Wt'], 'L1_attn_Wx': _L1_attn_in['Wx'], 'L1_attn_bh': _L1_attn_in['bh'], 'L1_attn_Wa': _L1_attn_in['Wa'], 'L1_attn_ba': _L1_attn_in['ba'], 'L1_ffn_gate_w': _L1_ffn_in['gate_w'], 'L1_ffn_gate_b': _L1_ffn_in['gate_b'], 'L1_ffn_w1': _L1_ffn_in['w1'], 'L1_ffn_b1': _L1_ffn_in['b1'], 'L1_ffn_w2': _L1_ffn_in['w2'], 'L1_ffn_b2': _L1_ffn_in['b2']}

def reference(x, L0_conv_qkv_w, L0_conv_qkv_b, L0_conv_rpb, L0_conv_proj_w, L0_conv_proj_b, L0_conv_g1_w, L0_conv_g1_b, L0_conv_g2_w, L0_conv_g2_b, L0_conv_ln_g, L0_conv_ln_b, L1_attn_Wt, L1_attn_Wx, L1_attn_bh, L1_attn_Wa, L1_attn_ba, L1_ffn_gate_w, L1_ffn_gate_b, L1_ffn_w1, L1_ffn_b1, L1_ffn_w2, L1_ffn_b2):
    import jax
    import jax.numpy as jnp

    def _L0_conv_ref(x, qkv_w, qkv_b, rpb, proj_w, proj_b, g1_w, g1_b, g2_w, g2_b, ln_g, ln_b):
        import jax, jax.numpy as jnp
        import numpy as np
        DIM, K, NH = (128, 7, 8)

        def _nbhd_idx(n, k):
            start = jnp.clip(jnp.arange(n) - k // 2, 0, n - k)
            idx = start[:, None] + jnp.arange(k)[None, :]
            bias = idx - jnp.arange(n)[:, None] + (k - 1)
            return (idx, bias)
        B, H, W, C = x.shape
        hd = C // NH
        scale = hd ** (-0.5)
        qkv = x @ qkv_w + qkv_b
        q, kk, v = jnp.split(qkv, 3, axis=-1)
        q = q.reshape(B, H, W, NH, hd) * scale
        kk = kk.reshape(B, H, W, NH, hd)
        v = v.reshape(B, H, W, NH, hd)
        ih, bh = _nbhd_idx(H, K)
        iw, bw = _nbhd_idx(W, K)
        kn = kk[:, ih][:, :, :, iw].transpose(0, 1, 3, 5, 2, 4, 6)
        vn = v[:, ih][:, :, :, iw].transpose(0, 1, 3, 5, 2, 4, 6)
        attn = jnp.einsum('bijnd,bijnpqd->bijnpq', q, kn)
        bias = rpb[:, bh][:, :, :, bw]
        bias = bias.transpose(1, 3, 0, 2, 4)
        attn = attn + bias[None]
        a = jax.nn.softmax(attn.reshape(B, H, W, NH, K * K), axis=-1)
        a = a.reshape(B, H, W, NH, K, K)
        out = jnp.einsum('bijnpq,bijnpqd->bijnd', a, vn).reshape(B, H, W, C)
        out = out @ proj_w + proj_b
        gate = jax.nn.sigmoid(jax.nn.relu(x @ g1_w + g1_b) @ g2_w + g2_b)
        y = x + out * gate
        mu = jnp.mean(y, axis=-1, keepdims=True)
        var = jnp.var(y, axis=-1, keepdims=True)
        return (y - mu) / jnp.sqrt(var + 1e-05) * ln_g + ln_b

    def _L1_attn_ref(inputs, Wt, Wx, bh, Wa, ba):
        import jax, jax.numpy as jnp
        import numpy as np
        B, L, D, U = (4, 512, 128, 32)
        q = jnp.einsum('bld,du->blu', inputs, Wt)
        k = jnp.einsum('bld,du->blu', inputs, Wx)
        h = jnp.tanh(q[:, :, None, :] + k[:, None, :, :] + bh)
        e = jnp.einsum('biju,u->bij', h, Wa[:, 0]) + ba[0]
        a = jax.nn.softmax(e, axis=-1)
        v = jnp.einsum('bij,bjd->bid', a, inputs)
        return v

    def _L1_ffn_ref(h, gate_w, gate_b, w1, b1, w2, b2):
        import math
        import jax, jax.numpy as jnp
        import numpy as np
        CAPACITY_FACTOR = 1.25
        B, L, D = h.shape
        E = gate_w.shape[1]
        T = B * L
        C = max(1, math.ceil(CAPACITY_FACTOR * T / E))
        x = h.reshape(T, D)
        logits = x @ gate_w + gate_b
        probs = jax.nn.softmax(logits, axis=-1)
        idx = jnp.argmax(probs, axis=-1)
        prb = jnp.take_along_axis(probs, idx[:, None], axis=1)[:, 0]
        one_hot = jax.nn.one_hot(idx, E, dtype=jnp.float32)
        pos = (jnp.cumsum(one_hot, axis=0) * one_hot).sum(-1).astype(jnp.int32) - 1
        kept = pos < C
        pos_safe = jnp.where(kept, pos, C)
        buf = jnp.zeros((E, C, D), dtype=h.dtype).at[idx, pos_safe].set(x, mode='drop')
        hmid = jax.nn.relu(jnp.einsum('ecd,edf->ecf', buf, w1) + b1[:, None, :])
        ybuf = jnp.einsum('ecf,efd->ecd', hmid, w2) + b2[:, None, :]
        pos_g = jnp.minimum(pos, C - 1)
        y_tok = ybuf[idx, pos_g] * (prb * kept)[:, None]
        y = y_tok.reshape(B, L, D)
        y = jnp.nan_to_num(y, nan=0.0, posinf=10000.0, neginf=-10000.0)
        return y

    def _gn(v, G=32, eps=1e-05):
        B_, H_, W_, C_ = v.shape
        g = v.reshape(B_, H_, W_, G, C_ // G)
        m = jnp.mean(g, axis=(1, 2, 4), keepdims=True)
        s = jnp.var(g, axis=(1, 2, 4), keepdims=True)
        return ((g - m) / jnp.sqrt(s + eps)).reshape(v.shape)

    def _ln_c(v, eps=1e-06):
        m = jnp.mean(v, axis=-1, keepdims=True)
        s = jnp.var(v, axis=-1, keepdims=True)
        return (v - m) / jnp.sqrt(s + eps)

    def _ln_t(v, eps=1e-05):
        m = jnp.mean(v, axis=-1, keepdims=True)
        s = jnp.var(v, axis=-1, keepdims=True)
        return (v - m) / jnp.sqrt(s + eps)

    def _to_tokens(v):
        B_, H_, W_, C_ = v.shape
        return v.reshape(B_, H_ * W_, C_)

    def _from_tokens(t, like):
        return t.reshape(like.shape)
    x = _L0_conv_ref(x, L0_conv_qkv_w, L0_conv_qkv_b, L0_conv_rpb, L0_conv_proj_w, L0_conv_proj_b, L0_conv_g1_w, L0_conv_g1_b, L0_conv_g2_w, L0_conv_g2_b, L0_conv_ln_g, L0_conv_ln_b)
    t = _to_tokens(x)
    t = t + _L1_attn_ref(_ln_t(t), L1_attn_Wt, L1_attn_Wx, L1_attn_bh, L1_attn_Wa, L1_attn_ba)
    t = t + _L1_ffn_ref(_ln_t(t), L1_ffn_gate_w, L1_ffn_gate_b, L1_ffn_w1, L1_ffn_b1, L1_ffn_w2, L1_ffn_b2)
    x = _from_tokens(t, x)
    return x

_drawn_inputs = setup_inputs


def setup_inputs(seed=0):
    import zlib

    import numpy as np

    out = dict(_drawn_inputs(seed))
    spreads = {'L0_conv_qkv_b': (0.0, 0.1),
     'L0_conv_proj_b': (0.0, 0.1),
     'L0_conv_g1_b': (0.0, 0.8),
     'L0_conv_ln_g': (1.0, 0.2),
     'L0_conv_ln_b': (0.0, 0.1),
     'L1_attn_bh': (0.0, 0.8),
     'L1_ffn_gate_b': (0.0, 0.1),
     'L1_ffn_b1': (0.0, 0.731),
     'L1_ffn_b2': (0.0, 0.51)}
    factors = {'L0_conv_rpb': 7.265}
    for name, (base, spread) in spreads.items():
        noise = np.random.default_rng([zlib.crc32(name.encode()), seed]).standard_normal(out[name].shape)
        drawn = base * np.exp(spread * noise) if base else spread * noise
        out[name] = jnp.asarray(drawn.astype(out[name].dtype))
    for name, factor in factors.items():
        out[name] = (out[name] * factor).astype(out[name].dtype)
    return out
```

```python
from contextlib import ExitStack

import numpy as np

import concourse.bass as bass
from concourse import mybir

F32 = mybir.dt.float32
BF16 = mybir.dt.bfloat16
I32 = mybir.dt.int32
U32 = mybir.dt.uint32
ALU = mybir.AluOpType
ACT = mybir.ActivationFunctionType
AX = mybir.AxisListType.X

P = 128
B, HT, WD, C = 2, 32, 32, 128
NT = B * HT * WD
L = HT * WD
ROWS = P // WD
NB = NT // P
BPI = NB // B
SLOTS = BPI + 2
KW_ = 7
HALO = KW_ // 2
NH, HD = 8, 16
WKEYS = (ROWS + 2 * HALO) * WD
WOFF = (ROWS - HALO) * WD
HP = 32
VW_COLS = NH * HP
U = 32
GH = C // 4
VG = VW_COLS + GH
QPG = P // U
CH = 8
NE, FF = 8, 512
FC = FF // P
CAP = -(-5 * NT // (4 * NE))
BIG = 1e30
FLT_MAX = float(np.finfo(np.float32).max)
SCALE = float(HD) ** -0.5

_COLS = [("wq", C), ("wk", C), ("wvg", VG), ("bvg", VG), ("g2w", GH), ("proj", 2 * C), ("projb", C),
         ("lng", C), ("lnb", C), ("wt", U), ("wx4", P), ("wa", 2 * U), ("gate", NE), ("gateb", NE),
         ("b1", NE * FC), ("b1e", NE * FC * NE), ("b2", C), ("bq", 1), ("bk", 1), ("g2b", 1),
         ("bh", 1), ("ba", 1), ("ident", P), ("tri", P), ("heads", NH), ("first", NE),
         ("pen", 3 * WKEYS)]
CST, _n = {}, 0
for _name, _w in _COLS:
    CST[_name] = (_n, _n + _w)
    _n += _w
CST_COLS = _n


class Chain:

    def __init__(self, eng, sem):
        self.eng, self.sem, self.n = eng, sem, 0

    def __call__(self, instruction):
        self.n += 1
        instruction.then_inc(self.sem, 1)
        self.eng.wait_ge(self.sem, self.n)

    def end(self):
        self.eng.sem_clear(self.sem)
        self.n = 0


def rsqrt(nc, link, y, v, w, iters=3):
    link(nc.vector.tensor_scalar(w.bitcast(I32), v.bitcast(I32), 1, None, ALU.arith_shift_right))
    link(nc.vector.tensor_scalar(y.bitcast(I32), w.bitcast(I32), -1.0, float(0x5F3759DF), ALU.mult, ALU.add))
    for _ in range(iters):
        link(nc.vector.tensor_tensor(w, y, y, ALU.mult))
        link(nc.vector.tensor_tensor(w, w, v, ALU.mult))
        link(nc.vector.tensor_scalar(w, w, -0.5, 1.5, ALU.mult, ALU.add))
        link(nc.vector.tensor_tensor(y, y, w, ALU.mult))


def program(nc, cst_d, xT_d, x_d, bias_d, w1_d, w2_d, out_d):
    with ExitStack() as ctx:
        def sb(name, shape, dt=F32):
            return ctx.enter_context(nc.sbuf_tensor(name, shape, dt))

        def sem(name):
            return ctx.enter_context(nc.semaphore(name))

        cst = sb("cst", [P, CST_COLS])

        def c_(name, lo=0, hi=None):
            a, b = CST[name]
            return cst[:, a + lo:(a + hi if hi is not None else b)]

        xT = sb("xT", [P, NT])
        x_all = sb("x_all", [P, NB, C])
        y_all = sb("y_all", [P, NB, C])
        kT = sb("kT", [P, B * SLOTS * P])
        qT = sb("qT", [P, NT])
        vg = sb("vg", [P, B * SLOTS, VG])
        gate = sb("gate", [P, NB])
        arena = sb("arena", [P, 4 * 4096])
        PW = 3 * P
        prob = [arena[:, i * NH * PW:(i + 1) * NH * PW].rearrange("p (h k) -> p h k", h=NH) for i in range(2)]
        o = 2 * NH * PW
        nlog = arena[:, o:o + NH * WKEYS].rearrange("p (h k) -> p h k", h=NH)
        o += NH * WKEYS
        btab = [arena[:, o + i * NH * WKEYS:o + (i + 1) * NH * WKEYS].rearrange("p (h k) -> p h k", h=NH)
                for i in range(2)]
        bias_in = nlog
        bottom = arena[:, 0:NH * WKEYS].rearrange("p (h k) -> p h k", h=NH)
        hid_ring = [arena[:, i * 4096:(i + 1) * 4096].rearrange("p (c j) -> p c j", c=4) for i in range(2)]
        w1 = arena[:, 8192:12288].rearrange("p (e f) -> p e f", e=NE)
        w2 = arena[:, 12288:16384].rearrange("p (e c d) -> p e c d", e=NE, c=FC)
        btab_d = [nc.dram_tensor(f"bias_table_{i}", (P, NH * WKEYS), F32).ap() for i in range(3)]

        qw = [sb(f"qw{i}", [P, P]) for i in range(2)]
        kw = [sb(f"kw{i}", [P, WKEYS]) for i in range(2)]
        vw = [sb(f"vw{i}", [P, 3, VW_COLS]) for i in range(2)]
        qm = [sb(f"qm{i}", [P, NH, P]) for i in range(2)]
        pts = [sb(f"pts{i}", [P, PW]) for i in range(2)]
        ots = sb("ots", [P, 2 * P])
        mn = [sb(f"mn{i}", [P, NH]) for i in range(2)]
        zs = [sb(f"zs{i}", [P, NH]) for i in range(2)]
        rz = [sb(f"rz{i}", [P, NH]) for i in range(2)]
        ytmp = sb("ytmp", [P, C])
        nbq = sb("nbq", [P, 1])
        hg2b = sb("hg2b", [P, 1])
        gz = sb("gz", [P, NB])
        gt = sb("gt", [P, NB])

        kcur = [sb(f"kcur{i}", [P, L]) for i in range(2)]
        xcur = [sb(f"xcur{i}", [P, BPI * C]) for i in range(2)]
        qcur = [sb(f"qcur{i}", [P, U]) for i in range(2)]
        nwa = sb("nwa", [P, 2 * U])
        trib = sb("trib", [P, P], BF16)
        oneb = sb("oneb", [P, P], BF16)
        nb1 = sb("nb1", [P, NE * FC])
        cexp = sb("cexp", [NE, C])
        pm = sb("pm", [P, L])
        ptm = sb("ptm", [P, BPI, P])
        nmin = sb("nmin", [P, 1])
        zm = sb("zm", [P, 1])
        rzm = sb("rzm", [P, 1])
        t2 = [sb(f"t2_{i}", [P, C]) for i in range(2)]
        xn = sb("xn", [P, C])
        xnT = [sb(f"xnT{i}", [P, P]) for i in range(2)]
        stats = sb("stats", [P, 6])
        mv = sb("mv", [P, 2])
        sv = sb("sv", [P, NB])
        sy = sb("sy", [P, NB])
        sw = sb("sw", [P, NB])
        mean = sb("mean", [P, NB])
        lg = sb("lg", [P, NE])
        mx = sb("mx", [P, 1])
        nmx = sb("nmx", [P, 1])
        lge = sb("lge", [P, NE])
        zg = sb("zg", [P, 1])
        prb = sb("prb", [P, 1])
        oha = sb("oha", [P, NE])
        ohw = sb("ohw", [P, 1])
        oh = sb("oh", [P, NE])
        ohb = sb("ohb", [P, NE], BF16)
        osum = sb("osum", [P, NE], BF16)
        keep = sb("keep", [P, NE])
        msk = [sb(f"msk{i}", [P, NE]) for i in range(2)]
        mT = sb("mT", [NE, P])
        hids = [sb(f"hids{i}", [P, FC, P]) for i in range(2)]
        acc = sb("acc", [P, C])
        bad = sb("bad", [P, 3, C], U32)
        fill = sb("fill", [P, 3, C])
        outs = [sb(f"outs{i}", [P, C]) for i in range(2)]

        ps = ctx.enter_context(nc.psum_tensor("ps", [P, 8 * 512], F32))

        def bank(i, lo=0, hi=512):
            return ps[:, 512 * i + lo:512 * i + hi]

        ld_cst, ld_xT, ld_x, ld_bias, ld_w = (sem(n) for n in ("ld_cst", "ld_xT", "ld_x", "ld_bias", "ld_w"))
        small_ready, pads_ready, margins_ready = sem("small_ready"), sem("pads_ready"), sem("margins_ready")
        btab_ready, btab_saved = sem("btab_ready"), sem("btab_saved")
        q_done, k_done, v_done = sem("q_done"), sem("k_done"), sem("v_done")
        q_ready, k_ready, v_ready = sem("q_ready"), sem("k_ready"), sem("v_ready")
        gz_ready, gt_ready = sem("gz_ready"), sem("gt_ready")
        qk_ld = [sem(f"qk_ld{i}") for i in range(2)]
        v_ld = [sem(f"v_ld{i}") for i in range(2)]
        bt_ld = [sem(f"bt_ld{i}") for i in range(2)]
        qm_ready, s_done, n_ready, p_ready = sem("qm_ready"), sem("s_done"), sem("n_ready"), sem("p_ready")
        rz_ready, pn_ready, pt_done = sem("rz_ready"), sem("pn_ready"), sem("pt_done")
        ptd_ready, pta_ready, pv_done = sem("ptd_ready"), sem("pta_ready"), sem("pv_done")
        ots_ready, proj_done, y_ready = sem("ots_ready"), sem("proj_done"), sem("y_ready")
        t_ready, tT_done, tT_ready = sem("t_ready"), sem("tT_done"), sem("tT_ready")
        k4_done, k4_ready, q4_done, q4_ready = sem("k4_done"), sem("k4_ready"), sem("q4_done"), sem("q4_ready")
        kq_ld = [sem(f"kq_ld{i}") for i in range(2)]
        xc_ld = [sem(f"xc_ld{i}") for i in range(2)]
        h_ready, h_used = sem("h_ready"), sem("h_used")
        nmin_ready, pm_ready = sem("nmin_ready"), sem("pm_ready")
        mt_done, mt_ready, pvm_done = sem("mt_done"), sem("mt_ready"), sem("pvm_done")
        xn_ready, xnT_done, xnT_ready = sem("xn_ready"), sem("xnT_done"), sem("xnT_ready")
        lg_done, mx_ready, ge_ready, oh_ready = sem("lg_done"), sem("mx_ready"), sem("ge_ready"), sem("oh_ready")
        cum_done, mask_ready = sem("cum_done"), sem("mask_ready")
        mT_done, mT_ready, ct_done, ct_used = sem("mT_done"), sem("mT_ready"), sem("ct_done"), sem("ct_used")
        hid_done, hid_ready, out_done, out_used = sem("hid_done"), sem("hid_ready"), sem("out_done"), sem("out_used")
        cx_done, cx_ready = sem("cx_done"), sem("cx_ready")
        fin_ready = sem("fin_ready")
        out_st = [sem(f"out_st{i}") for i in range(2)]
        dve_chain = sem("dve_chain")
        passed_dve, passed_pool = sem("passed_dve"), sem("passed_pool")

        block = ctx.enter_context(nc.Block())

        @block.sync
        def _(sp):
            sp.dma_start(cst[:, :], cst_d).then_inc(ld_cst, 16)
            sp.dma_start(xT[:, :], xT_d).then_inc(ld_xT, 16)
            sp.dma_start(bias_in, bias_d.rearrange("p (h k) -> p h k", h=NH)).then_inc(ld_bias, 16)
            sp.dma_start(x_all[:, :, :], x_d.rearrange("(n p) c -> p n c", p=P)).then_inc(ld_x, 16)
            flat = [btab[0], btab[1], bottom]
            for i in range(3):
                sp.wait_ge(btab_ready, i + 1)
                sp.dma_start(btab_d[i], flat[i].rearrange("p h k -> p (h k)")).then_inc(btab_saved, 16)
            sp.wait_ge(btab_saved, 48)
            sp.wait_ge(q_ready, 4)
            sp.wait_ge(k_ready, 4)
            sp.wait_ge(v_ready, NB)
            sp.wait_ge(pads_ready, 2)
            kind_of = lambda j: 0 if j % BPI == 0 else 2 if j % BPI == BPI - 1 else 1
            held = [0, 1]
            for j in range(NB):
                par, slot = j % 2, j + 2 * (j // BPI)
                if j >= 2:
                    sp.wait_ge(s_done, NH * (j - 1))
                sp.dma_start(qw[par][:, :], qT[:, j * P:(j + 1) * P]).then_inc(qk_ld[par], 16)
                sp.dma_start(kw[par][:, :], kT[:, slot * P + WOFF:slot * P + WOFF + WKEYS]).then_inc(qk_ld[par], 16)
                if kind_of(j) != held[par]:
                    held[par] = kind_of(j)
                    sp.wait_ge(n_ready, NH * (j - 1))
                    sp.dma_start(btab[par].rearrange("p h k -> p (h k)"), btab_d[held[par]]).then_inc(bt_ld[par], 16)
                if j >= 2:
                    sp.wait_ge(pv_done, NH * (j - 1))
                sp.dma_start(vw[par][:, :, :], vg[:, slot:slot + 3, 0:VW_COLS]).then_inc(v_ld[par], 16)
            sp.wait_ge(pt_done, NH * NB)
            sp.wait_ge(n_ready, NH * NB)
            sp.wait_ge(p_ready, NH * NB)
            sp.dma_start(w1, w1_d.rearrange("p (e f) -> p e f", e=NE)).then_inc(ld_w, 16)
            sp.dma_start(w2, w2_d.rearrange("p (e c d) -> p e c d", e=NE, c=FC)).then_inc(ld_w, 16)

            sp.wait_ge(t_ready, 1)
            sp.wait_ge(k4_ready, 4)
            sp.wait_ge(q4_ready, 1)

            def stage(i, par, img):
                sp.dma_start(kcur[par][:, :], kT[:, img * L:(img + 1) * L]).then_inc(kq_ld[par], 16)
                sp.dma_start(qcur[par][:, :], qT[:, bass.ds(i * U, U)]).then_inc(kq_ld[par], 16)
                src = x_all[:, img * BPI:(img + 1) * BPI, :].rearrange("p n c -> p (n c)")
                sp.dma_start(xcur[par][:, :], src).then_inc(xc_ld[par], 16)

            def store(i, par):
                sp.wait_ge(fin_ready, i + 1)
                sp.dma_start(out_d[bass.ds(i * P, P), :], outs[par][:, :]).then_inc(out_st[par], 16)

            def turn(i, par, img, stores=True):
                sp.wait_ge(h_ready, CH * (i - 1))
                sp.wait_ge(pvm_done, i - 1)
                stage(i, par, img)
                if stores:
                    store(i - 3, 1 - par)

            stage(0, 0, 0)
            stage(1, 1, 0)
            turn(2, 0, 0, stores=False)
            for i in (3, 4, 5, 6, 7):
                turn(i, i % 2, 0)
            with sp.Fori(BPI // 2, NB // 2) as n:
                for par in range(2):
                    turn(2 * n + par, par, 1)
            for i in range(NB - 3, NB):
                store(i, i % 2)
            sp.wait_ge(out_st[0], 16 * NB // 2)
            sp.wait_ge(out_st[1], 16 * NB // 2)

        @block.gpsimd
        def _(pool):
            for b in range(B):
                for s in (0, SLOTS - 1):
                    at = b * SLOTS + s
                    nc.gpsimd.memset(kT[:, at * P:(at + 1) * P], 0.0)
                    last = nc.gpsimd.memset(vg[:, at, :], 0.0)
                last.then_inc(pads_ready, 1)
            pool.wait_ge(btab_saved, 48)
            for t in prob:
                nc.gpsimd.memset(t[:, :, 0:WOFF], 0.0)
                last = nc.gpsimd.memset(t[:, :, WOFF + WKEYS:PW], 0.0)
            last.then_inc(margins_ready, 1)

            def mask_heads(j, par, first=False):
                if not first:
                    pool.wait_ge(s_done, NH * (j - 1))
                pool.wait_ge(qk_ld[par], 16 * (j - par + 2))
                nc.gpsimd.tensor_tensor(qm[par][:, :, :], qw[par][:, None, :].broadcast_to([P, NH, P]),
                                        c_("heads")[:, :, None].broadcast_to([P, NH, P]),
                                        ALU.mult).then_inc(qm_ready, 1)

            def normalise(j, par, h0, h1):
                pool.wait_ge(rz_ready, j + 1)
                pool.sem_inc(passed_pool, 1)
                for h in range(h0, h1):
                    nc.gpsimd.tensor_scalar(prob[par][:, h, WOFF:WOFF + WKEYS], prob[par][:, h, WOFF:WOFF + WKEYS],
                                            rz[par][:, h:h + 1], 1.0, ALU.mult, ALU.mult).then_inc(pn_ready, 1)

            def step(j, par, more=True):
                normalise(j - 1, 1 - par, 0, 4)
                if more:
                    mask_heads(j + 1, 1 - par)
                normalise(j - 1, 1 - par, 4, NH)

            pool.wait_ge(ld_cst, 16)
            mask_heads(0, 0, first=True)
            mask_heads(1, 1, first=True)
            step(1, 1)
            with pool.Fori(1, NB // 2 - 1) as n:
                for par in range(2):
                    step(2 * n + par, par)
            step(NB - 2, 0)
            step(NB - 1, 1, more=False)
            step(NB, 0, more=False)

        @block.tensor
        def _(pe):
            pe.wait_ge(ld_cst, 16)
            pe.wait_ge(ld_xT, 16)
            for i in range(4):
                if i >= 2:
                    pe.wait_ge(q_ready, i - 1)
                nc.tensor.matmul(bank(i % 2), c_("wq"), xT[:, i * 512:(i + 1) * 512],
                                 start=True, stop=True).then_inc(q_done, 1)
                if i >= 2:
                    pe.wait_ge(k_ready, i - 1)
                nc.tensor.matmul(bank(2 + i % 2), c_("wk"), xT[:, i * 512:(i + 1) * 512],
                                 start=True, stop=True).then_inc(k_done, 1)
            for i in range(NB):
                if i >= 4:
                    pe.wait_ge(v_ready, i - 3)
                nc.tensor.matmul(bank(4 + i % 4, 0, VG), xT[:, i * P:(i + 1) * P], c_("wvg"),
                                 start=True, stop=True).then_inc(v_done, 1)
            pe.wait_ge(q_ready, 4)
            pe.wait_ge(k_ready, 4)
            pe.wait_ge(v_ready, NB)

            def scores(j, par, h):
                if h == 0:
                    pe.wait_ge(qm_ready, j + 1)
                    pe.wait_ge(qk_ld[par], 16 * (j - par + 2))
                if h >= 4 or not (isinstance(j, int) and j == 0):
                    pe.wait_ge(n_ready, NH * j + h - 3)
                nc.tensor.matmul(bank(h % 4, 0, WKEYS), qm[par][:, h, :], kw[par][:, :],
                                 start=True, stop=True).then_inc(s_done, 1)

            def turn_probs(j, par, h):
                pe.wait_ge(pn_ready, NH * j + h + 1)
                if h >= 2 or not (isinstance(j, int) and j == 0):
                    pe.wait_ge(pta_ready if h % 2 else ptd_ready, NH // 2 * j + h // 2)
                for k in range(3):
                    last = nc.tensor.transpose(bank(4 + h % 2, k * P, (k + 1) * P),
                                               prob[par][:, h, k * P:(k + 1) * P], c_("ident"))
                last.then_inc(pt_done, 1)

            def values(j, par, h):
                if h == 0:
                    pe.wait_ge(v_ld[par], 8 * (j - par + 2))
                    if not (isinstance(j, int) and j == 0):
                        pe.wait_ge(ots_ready, j)
                pe.wait_ge(pta_ready if h % 2 else ptd_ready, NH // 2 * j + h // 2 + 1)
                g, half = h % 4, h // 4
                for k in range(3):
                    last = nc.tensor.matmul(bank(6, half * P, (half + 1) * P)[g * HP:(g + 1) * HP, :],
                                            vw[par][:, k, h * HP:(h + 1) * HP],
                                            pts[h % 2][:, k * P:(k + 1) * P], start=(k == 0), stop=(k == 2))
                last.then_inc(pv_done, 1)

            def project(j):
                pe.wait_ge(ots_ready, j + 1)
                if not (isinstance(j, int) and j == 0):
                    pe.wait_ge(y_ready, j)
                for half in range(2):
                    last = nc.tensor.matmul(bank(7, 0, C), ots[:, half * P:(half + 1) * P],
                                            c_("proj", half * C, (half + 1) * C), start=(half == 0), stop=(half == 1))
                last.then_inc(proj_done, 1)

            def step(j, par, score=True, value=True, proj=True):
                for i in range(NH + 2):
                    if score and i < NH:
                        scores(j, par, i)
                    if proj and i == 1:
                        project(j - 2)
                    if value and 1 <= i <= NH:
                        turn_probs(j - 1, 1 - par, i - 1)
                    if value and i >= 2:
                        values(j - 1, 1 - par, i - 2)

            pe.wait_ge(margins_ready, 1)
            step(0, 0, value=False, proj=False)
            step(1, 1, proj=False)
            with pe.Fori(1, NB // 2) as n:
                for par in range(2):
                    step(2 * n + par, par)
            step(NB, 0, score=False)
            project(NB - 1)

            pe.wait_ge(t_ready, 1)
            for i in range(4):
                for k in range(4):
                    last = nc.tensor.transpose(bank(i, k * P, (k + 1) * P), x_all[:, 4 * i + k, :], c_("ident"))
                last.then_inc(tT_done, 1)
            for i in range(4):
                pe.wait_ge(tT_ready, i + 1)
                nc.tensor.matmul(bank(4 + i), c_("wx4"), xT[:, i * 512:(i + 1) * 512],
                                 start=True, stop=True).then_inc(k4_done, 1)
            by4 = xT[:, :].rearrange("p (m g) -> p g m", g=QPG)
            for g in range(QPG):
                last = nc.tensor.matmul(bank(0)[g * U:(g + 1) * U, :], c_("wt"), by4[:, g, :], start=True, stop=True)
            last.then_inc(q4_done, 1)
            pe.wait_ge(q4_ready, 1)
            pe.wait_ge(k4_ready, 4)

            def energies(i, par, s):
                pe.wait_ge(h_ready, CH * i + s + 1)
                if s == 0 and not (isinstance(i, int) and i < 2):
                    pe.wait_ge(pm_ready, i - 1)
                for half in range(2):
                    for c in range(4):
                        last = nc.tensor.matmul(bank(2 * par + half)[c * U:(c + 1) * U, :],
                                                nwa[:, U - QPG - QPG * s:2 * U - QPG - QPG * s],
                                                hid_ring[s % 2][:, c, half * 512:(half + 1) * 512],
                                                start=(s == 0), stop=(s == CH - 1))
                last.then_inc(h_used, 1)

            def turn_main(i, half):
                if half == 0:
                    pe.wait_ge(pm_ready, i + 1)
                if half or not (isinstance(i, int) and i == 0):
                    pe.wait_ge(mt_ready, 2 * i + half)
                for k in range(4):
                    last = nc.tensor.transpose(bank(4, k * P, (k + 1) * P),
                                               pm[:, (4 * half + k) * P:(4 * half + k + 1) * P], c_("ident"))
                last.then_inc(mt_done, 1)

            def attend(i, par, after_experts):
                pe.wait_ge(mt_ready, 2 * i + 2)
                pe.wait_ge(xc_ld[par], 8 * (i - par + 2))
                if after_experts:
                    pe.wait_ge(ct_used, i)
                for k in range(BPI):
                    last = nc.tensor.matmul(bank(5, 0, C), ptm[:, k, :], xcur[par][:, k * C:(k + 1) * C],
                                            start=(k == 0), stop=(k == BPI - 1))
                last.then_inc(pvm_done, 1)

            def hidden(i, par, e):
                if e == 0:
                    pe.wait_ge(xnT_ready, i + 1)
                if e or not (isinstance(i, int) and i == 0):
                    pe.wait_ge(hid_ready, NE * i + e)
                for c in range(FC):
                    last = nc.tensor.matmul(bank(6, c * P, (c + 1) * P), w1[:, e, c * P:(c + 1) * P], xnT[par][:, :],
                                            start=True, stop=True)
                last.then_inc(hid_done, 1)

            def expert(i, e):
                pe.wait_ge(hid_ready, NE * i + e + 1)
                if e or not (isinstance(i, int) and i == 0):
                    pe.wait_ge(out_used, NE * i + e)
                for c in range(FC):
                    last = nc.tensor.matmul(bank(7, 0, C), hids[e % 2][:, c, :], w2[:, e, c, :],
                                            start=(c == 0), stop=(c == FC - 1))
                last.then_inc(out_done, 1)

            def step_main(i, par, energy=True, attn=True, moe=True):
                p, q = i - 1, i - 2
                for s in range(CH):
                    if s == 0 and moe:
                        pe.wait_ge(mask_ready, q + 1)
                        nc.tensor.transpose(bank(5, 0, P)[0:NE, :], msk[par][:, :], c_("ident")).then_inc(mT_done, 1)
                    if s == 1 and moe:
                        pe.wait_ge(mT_ready, q + 1)
                        nc.tensor.matmul(bank(5, 0, C), mT[:, :], cexp[:, :], start=True, stop=True).then_inc(ct_done, 1)
                    if attn and s in (1, 2):
                        turn_main(p, s - 1)
                    if attn and s == 3:
                        attend(p, 1 - par, moe)
                    if attn and s == 5:
                        pe.wait_ge(xn_ready, p + 1)
                        nc.tensor.transpose(bank(5, 0, P), xn[:, :], c_("ident")).then_inc(xnT_done, 1)
                    if attn and s == 6:
                        pe.wait_ge(xnT_ready, p + 1)
                        nc.tensor.matmul(bank(5, 0, NE), xnT[1 - par][:, :], c_("gate"),
                                         start=True, stop=True).then_inc(lg_done, 1)
                    if attn and s == 7:
                        pe.wait_ge(oh_ready, p + 1)
                        nc.tensor.matmul(bank(5, 0, NE), trib[:, :], ohb[:, :], start=True, stop=False)
                        nc.tensor.matmul(bank(5, 0, NE), oneb[:, :], osum[:, :], start=False, stop=True).then_inc(cum_done, 1)
                    if moe and s < CH - 1:
                        hidden(q, par, s + 1)
                    if attn and s == CH - 1:
                        hidden(p, 1 - par, 0)
                    if energy:
                        energies(i, par, s)
                    if moe and s < CH - 1:
                        expert(q, s + 1)
                    if attn and s == CH - 1:
                        expert(p, 0)

            step_main(0, 0, attn=False, moe=False)
            pe.wait_ge(ld_w, 32)
            for e in range(NE):
                for c in range(FC):
                    k = e * FC + c
                    last = nc.tensor.matmul(bank(7, 0, C)[0:NE, :], c_("b1e", k * NE, (k + 1) * NE), w2[:, e, c, :],
                                            start=(k == 0), stop=(k == NE * FC - 1))
            last.then_inc(cx_done, 1)
            pe.wait_ge(cx_ready, 1)
            step_main(1, 1, moe=False)
            with pe.Fori(1, NB // 2) as n:
                for par in range(2):
                    step_main(2 * n + par, par)
            step_main(NB, 0, energy=False)
            step_main(NB + 1, 1, energy=False, attn=False)

        @block.scalar
        def _(act):
            act.wait_ge(small_ready, 1)
            for i in range(4):
                act.wait_ge(q_done, i + 1)
                nc.scalar.activation(qT[:, i * 512:(i + 1) * 512], bank(i % 2), ACT.Identity,
                                     bias=nbq[:, :], scale=-SCALE).then_inc(q_ready, 1)
            act.wait_ge(gz_ready, 1)
            nc.scalar.activation(gt[:, :], gz[:, :], ACT.Tanh, bias=hg2b[:, :], scale=0.5).then_inc(gt_ready, 1)
            act.wait_ge(margins_ready, 1)

            def soften(j, par, h):
                act.wait_ge(n_ready, NH * j + h + 1)
                if h == 0 and not (isinstance(j, int) and j < 2):
                    act.wait_ge(pt_done, NH * (j - 1))
                nc.scalar.activation(prob[par][:, h, WOFF:WOFF + WKEYS], nlog[:, h, :], ACT.Exp,
                                     bias=mn[par][:, h:h + 1], scale=-1.0,
                                     accum_out=zs[par][:, h:h + 1]).then_inc(p_ready, 1)

            def turned(j, h):
                act.wait_ge(pt_done, NH * j + h + 1)
                if h >= 2 or not (isinstance(j, int) and j == 0):
                    act.wait_ge(pv_done, NH * j + h - 1)
                nc.scalar.activation(pts[1][:, :], bank(5, 0, PW), ACT.Copy).then_inc(pta_ready, 1)

            def heads_out(j):
                act.wait_ge(pv_done, NH * (j + 1))
                if not (isinstance(j, int) and j == 0):
                    act.wait_ge(proj_done, j)
                nc.scalar.activation(ots[:, :], bank(6, 0, 2 * P), ACT.Copy).then_inc(ots_ready, 1)

            def step(j, par, score=True, value=True):
                for i in range(NH + 1):
                    if score and i < NH:
                        soften(j, par, i)
                    if value and i >= 2 and i % 2 == 0:
                        turned(j - 1, i - 1)
                if value:
                    heads_out(j - 1)

            step(0, 0, value=False)
            step(1, 1)
            with act.Fori(1, NB // 2) as n:
                for par in range(2):
                    step(2 * n + par, par)
            step(NB, 0, score=False)

            for i in range(4):
                act.wait_ge(tT_done, i + 1)
                nc.scalar.activation(xT[:, i * 512:(i + 1) * 512], bank(i), ACT.Copy).then_inc(tT_ready, 1)
            for i in range(4):
                act.wait_ge(k4_done, i + 1)
                nc.scalar.activation(kT[:, i * 512:(i + 1) * 512], bank(4 + i), ACT.Identity,
                                     bias=c_("bh")).then_inc(k4_ready, 1)

            def hidden_units(i, par, s):
                if s == 0:
                    act.wait_ge(kq_ld[par], 16 * (i - par + 2))
                if s >= 2 or not (isinstance(i, int) and i == 0):
                    act.wait_ge(h_used, CH * i + s - 1)
                for c in range(4):
                    m = c * CH + s
                    last = nc.scalar.activation(hid_ring[s % 2][:, c, :], kcur[par][:, :], ACT.Tanh,
                                                bias=qcur[par][:, m:m + 1])
                last.then_inc(h_ready, 1)

            def soften_main(i, par):
                act.wait_ge(nmin_ready, i + 1)
                if not (isinstance(i, int) and i == 0):
                    act.wait_ge(mt_done, 2 * i)
                nc.scalar.activation(pm[:, :], ps[:, par * L:(par + 1) * L], ACT.Exp, bias=nmin[:, :], scale=-1.0,
                                     accum_out=zm[:, :]).then_inc(pm_ready, 1)

            def step_main(i, par, energy=True, attn=True):
                for s in range(CH):
                    if energy:
                        hidden_units(i, par, s)
                    if attn and s == 0:
                        soften_main(i - 1, 1 - par)
                    if attn and s == 6:
                        act.wait_ge(mx_ready, i)
                        nc.scalar.activation(lge[:, :], lg[:, :], ACT.Exp, bias=nmx[:, :],
                                             accum_out=zg[:, :]).then_inc(ge_ready, 1)

            step_main(0, 0, attn=False)
            step_main(1, 1)
            with act.Fori(1, NB // 2) as n:
                for par in range(2):
                    step_main(2 * n + par, par)
            step_main(NB, 0, energy=False)

        @block.vector
        def _(dve):
            link = Chain(dve, dve_chain)
            dve.wait_ge(ld_cst, 16)
            nc.vector.tensor_scalar(hg2b[:, :], c_("g2b"), 0.5, None, ALU.mult)
            nc.vector.tensor_scalar(nwa[:, :], c_("wa"), -1.0, None, ALU.mult)
            nc.vector.tensor_copy(trib[:, :], c_("tri"))
            nc.vector.memset(oneb[:, :], 1.0)
            nc.vector.memset(osum[:, :], 0.0)
            nc.vector.tensor_scalar(nb1[:, :], c_("b1"), -1.0, None, ALU.mult)
            for i, v in enumerate((0.0, 1e4, -1e4)):
                nc.vector.memset(fill[:, i, :], v)
            nc.vector.tensor_scalar(nbq[:, :], c_("bq"), -SCALE, None, ALU.mult).then_inc(small_ready, 1)

            def key_rows(i):
                dve.wait_ge(k_done, i + 1)
                at = (i // 2) * SLOTS * P + P + (i % 2) * 512
                nc.vector.tensor_scalar(kT[:, at:at + 512], bank(2 + i % 2), c_("bk"), None, ALU.add).then_inc(k_ready, 1)

            for i in range(4):
                key_rows(i)
            for i in range(NB):
                dve.wait_ge(v_done, i + 1)
                nc.vector.tensor_tensor(vg[:, i + 1 + 2 * (i // BPI), :], bank(4 + i % 4, 0, VG), c_("bvg"),
                                        ALU.add).then_inc(v_ready, 1)
            dve.wait_ge(ld_bias, 16)
            for i, t in enumerate((btab[0], btab[1], bottom)):
                nc.vector.tensor_tensor(t, c_("pen", i * WKEYS, (i + 1) * WKEYS)[:, None, :].broadcast_to([P, NH, WKEYS]),
                                        bias_in, ALU.subtract).then_inc(btab_ready, 1)
            dve.wait_ge(btab_ready, 3)
            dve.wait_ge(v_ready, NB)
            for b in range(B):
                hid = vg[:, b * SLOTS + 1:b * SLOTS + 1 + BPI, VW_COLS:VG]
                g2 = c_("g2w")[:, None, :].broadcast_to([P, BPI, GH])
                link(nc.vector.scalar_tensor_tensor(hid, hid, 0.0, g2, ALU.max, ALU.mult))
                link(nc.vector.tensor_reduce(gz[:, b * BPI:(b + 1) * BPI], hid, AX, ALU.add))
            link.end()
            nc.vector.drain().then_inc(gz_ready, 1)
            dve.wait_ge(gt_ready, 1)
            link(nc.vector.tensor_scalar(gate[:, :], gt[:, :], 0.5, 0.5, ALU.mult, ALU.add))
            link.end()

            def bias_scores(j, par, h, table):
                if h == 0 and table is not None:
                    dve.wait_ge(bt_ld[par], table)
                dve.wait_ge(s_done, NH * j + h + 1)
                if not (isinstance(j, int) and j == 0):
                    dve.wait_ge(p_ready, NH * (j - 1) + h + 1)
                dve.sem_inc(passed_dve, 1)
                nc.vector.tensor_tensor_reduce(out=nlog[:, h, :], in0=bank(h % 4, 0, WKEYS), in1=btab[par][:, h, :],
                                               scale=1.0, scalar=3e38, op0=ALU.add, op1=ALU.min,
                                               accum_out=mn[par][:, h:h + 1]).then_inc(n_ready, 1)

            def norms(j, par):
                dve.wait_ge(p_ready, NH * (j + 1))
                nc.vector.reciprocal(rz[par][:, :], zs[par][:, :]).then_inc(rz_ready, 1)

            def turned(j, h):
                dve.wait_ge(pt_done, NH * j + h + 1)
                if h >= 2 or not (isinstance(j, int) and j == 0):
                    dve.wait_ge(pv_done, NH * j + h - 1)
                nc.vector.tensor_copy(pts[0][:, :], bank(4, 0, PW)).then_inc(ptd_ready, 1)

            def gated(j):
                dve.wait_ge(proj_done, j + 1)
                link(nc.vector.tensor_tensor(ytmp[:, :], bank(7, 0, C), c_("projb"), ALU.add))
                sq = lambda t: t[:, j, :] if isinstance(j, int) else t[:, bass.ds(j, 1), :].rearrange("p n c -> p (n c)")
                g = gate[:, j:j + 1] if isinstance(j, int) else gate[:, bass.ds(j, 1)]
                link(nc.vector.scalar_tensor_tensor(sq(y_all), ytmp[:, :], g, sq(x_all), ALU.mult, ALU.add))
                link.end()
                dve.sem_inc(y_ready, 1)

            def step(j, par, score=True, value=True, proj=True, table=None):
                for i in range(NH + 1):
                    if score and i < NH:
                        bias_scores(j, par, i, table)
                    if value and i == 1:
                        norms(j - 1, 1 - par)
                    if proj and i == 3:
                        gated(j - 2)
                    if value and i >= 1 and i % 2 == 1:
                        turned(j - 1, i - 1)

            def loads_of(j):
                return 16 * sum(k <= j for k in ((2, 8, 10) if j % 2 == 0 else (7, 9, 15)))

            dve.wait_ge(ld_x, 16)
            step(0, 0, value=False, proj=False)
            step(1, 1, proj=False)
            step(2, 0, table=loads_of(2))
            for lo, hi in ((3, 7), (11, 15)):
                if lo == 11:
                    for j in (7, 8, 9, 10):
                        step(j, j % 2, table=loads_of(j))
                with dve.Fori(0, (hi - lo) // 2) as n:
                    for k in range(2):
                        step(2 * n + lo + k, (lo + k) % 2)
            step(NB - 1, 1, table=loads_of(NB - 1))
            step(NB, 0, score=False)
            gated(NB - 1)
            dve.wait_ge(y_ready, NB)

            wide = lambda t: t[:, :].unsqueeze(2).broadcast_to([P, NB, C]) if hasattr(t[:, :], "unsqueeze") else t[:, :, None].broadcast_to([P, NB, C])
            row = lambda n: c_(n)[:, None, :].broadcast_to([P, NB, C])

            def norm(dst, src, scratch):
                link(nc.vector.tensor_reduce(mean[:, :], src, AX, ALU.add))
                link(nc.vector.tensor_scalar(mean[:, :], mean[:, :], 1.0 / C, None, ALU.mult))
                link(nc.vector.tensor_tensor(dst, src, mean[:, :, None].broadcast_to([P, NB, C]), ALU.subtract))
                link(nc.vector.tensor_tensor(scratch, dst, dst, ALU.mult))
                link(nc.vector.tensor_reduce(sv[:, :], scratch, AX, ALU.add))
                link(nc.vector.tensor_scalar(sv[:, :], sv[:, :], 1.0 / C, 1e-5, ALU.mult, ALU.add))
                rsqrt(nc, link, sy[:, :], sv[:, :], sw[:, :])
                link(nc.vector.tensor_tensor(dst, dst, sy[:, :, None].broadcast_to([P, NB, C]), ALU.mult))

            y3, x3 = y_all[:, :, :], x_all[:, :, :]
            scratch = xT[:, :].rearrange("p (n c) -> p n c", n=NB)
            norm(y3, y3, scratch)
            link(nc.vector.tensor_tensor(y3, y3, row("lng"), ALU.mult))
            link(nc.vector.tensor_tensor(y3, y3, row("lnb"), ALU.add))
            norm(x3, y3, scratch)
            link.end()
            dve.sem_inc(t_ready, 1)
            dve.wait_ge(q4_done, 1)
            nc.vector.tensor_copy(qT[:, 0:NT // QPG], bank(0)).then_inc(q4_ready, 1)

            def least(i, par):
                dve.wait_ge(h_used, CH * (i + 1))
                link(nc.vector.tensor_reduce(nmin[:, :], ps[:, par * L:(par + 1) * L], AX, ALU.min))
                nc.vector.tensor_scalar(nmin[:, :], nmin[:, :], c_("ba"), c_("ba"), ALU.subtract, ALU.add).then_inc(nmin_ready, 1)
                link.end()

            def turned_main(i, half):
                dve.wait_ge(mt_done, 2 * i + half + 1)
                if half == 0 and not (isinstance(i, int) and i == 0):
                    dve.wait_ge(pvm_done, i)
                nc.vector.tensor_copy(ptm[:, 4 * half:4 * half + 4, :].rearrange("p k q -> p (k q)"),
                                      bank(4)).then_inc(mt_ready, 1)

            def attended(i, par):
                dve.wait_ge(pvm_done, i + 1)
                link(nc.vector.reciprocal(rzm[:, :], zm[:, :]))
                t = y_all[:, i, :] if isinstance(i, int) else y_all[:, bass.ds(i, 1), :].rearrange("p n c -> p (n c)")
                link(nc.vector.scalar_tensor_tensor(t2[par][:, :], bank(5, 0, C), rzm[:, :], t, ALU.mult, ALU.add))
                link(nc.vector.bn_stats(stats[:, :], t2[par][:, :]))
                link(nc.vector.bn_aggr(mv[:, :], stats[:, :]))
                link(nc.vector.tensor_scalar(sv[:, 0:1], mv[:, 1:2], 1e-5, None, ALU.add))
                rsqrt(nc, link, sy[:, 0:1], sv[:, 0:1], sw[:, 0:1])
                nc.vector.tensor_scalar(xn[:, :], t2[par][:, :], mv[:, 0:1], sy[:, 0:1], ALU.subtract,
                                        ALU.mult).then_inc(xn_ready, 1)
                link.end()

            def route(i):
                dve.wait_ge(lg_done, i + 1)
                link(nc.vector.tensor_tensor(lg[:, :], bank(5, 0, NE), c_("gateb"), ALU.add))
                link(nc.vector.tensor_reduce(mx[:, :], lg[:, :], AX, ALU.max))
                nc.vector.tensor_scalar(nmx[:, :], mx[:, :], -1.0, None, ALU.mult).then_inc(mx_ready, 1)
                link(nc.vector.tensor_scalar(oha[:, :], lg[:, :], mx[:, :], None, ALU.is_equal))
                link(nc.vector.tensor_tensor(oha[:, :], oha[:, :], c_("first"), ALU.mult))
                link(nc.vector.tensor_reduce(ohw[:, :], oha[:, :], AX, ALU.max))
                link(nc.vector.tensor_scalar(oh[:, :], oha[:, :], ohw[:, :], None, ALU.is_equal))
                nc.vector.tensor_copy(ohb[:, :], oh[:, :]).then_inc(oh_ready, 1)
                link.end()

            def weigh(i, par):
                dve.wait_ge(cum_done, i + 1)
                dve.wait_ge(ge_ready, i + 1)
                link(nc.vector.reciprocal(prb[:, :], zg[:, :]))
                link(nc.vector.tensor_scalar(keep[:, :], bank(5, 0, NE), CAP + 0.5, prb[:, :], ALU.is_lt, ALU.mult))
                link(nc.vector.tensor_tensor(osum[:, :], osum[:, :], ohb[:, :], ALU.add))
                nc.vector.tensor_tensor(msk[par][:, :], keep[:, :], oh[:, :], ALU.mult).then_inc(mask_ready, 1)
                link.end()

            def hidden(i, e):
                dve.wait_ge(hid_done, NE * i + e + 1)
                if e >= 2 or not (isinstance(i, int) and i == 0):
                    dve.wait_ge(out_done, NE * i + e - 1)
                nc.vector.tensor_tensor(hids[e % 2][:, :, :], bank(6).rearrange("p (c t) -> p c t", c=FC),
                                        nb1[:, e * FC:(e + 1) * FC, None].broadcast_to([P, FC, P]),
                                        ALU.max).then_inc(hid_ready, 1)

            def combine(i, par, e):
                dve.wait_ge(out_done, NE * i + e + 1)
                w = msk[par][:, e:e + 1]
                if e == 0:
                    dve.wait_ge(mask_ready, i + 1)
                    if not (isinstance(i, int) and i == 0):
                        dve.wait_ge(fin_ready, i)
                    nc.vector.tensor_scalar(acc[:, :], bank(7, 0, C), w, None, ALU.mult).then_inc(out_used, 1)
                else:
                    dve.wait_ge(out_used, NE * i + e)
                    nc.vector.scalar_tensor_tensor(acc[:, :], bank(7, 0, C), w, acc[:, :], ALU.mult, ALU.add).then_inc(out_used, 1)

            def finish(i, par, first):
                dve.wait_ge(out_used, NE * (i + 1))
                if not first:
                    dve.wait_ge(out_st[par], 8 * (i - par))
                link(nc.vector.tensor_tensor(bad[:, 0, :], acc[:, :], acc[:, :], ALU.not_equal))
                link(nc.vector.tensor_scalar(bad[:, 1, :], acc[:, :], FLT_MAX, None, ALU.is_gt))
                link(nc.vector.tensor_scalar(bad[:, 2, :], acc[:, :], -FLT_MAX, None, ALU.is_lt))
                for k in range(3):
                    link(nc.vector.copy_predicated(acc[:, :], bad[:, k, :], fill[:, k, :]))
                nc.vector.tensor_tensor(outs[par][:, :], acc[:, :], t2[par][:, :], ALU.add).then_inc(fin_ready, 1)
                link.end()

            def step_main(i, par, energy=True, attn=True, moe=True):
                p, q = i - 1, i - 2
                for s in range(CH):
                    if moe:
                        combine(q, par, s)
                    if moe and s < CH - 1:
                        hidden(q, s + 1)
                    if attn and s == CH - 1:
                        hidden(p, 0)
                    if attn and s == 0:
                        least(p, 1 - par)
                    if moe and s == 0:
                        dve.wait_ge(mT_done, q + 1)
                        nc.vector.tensor_copy(mT[:, :], bank(5, 0, P)[0:NE, :]).then_inc(mT_ready, 1)
                    if moe and s == 1:
                        dve.wait_ge(ct_done, q + 1)
                        dve.wait_ge(out_used, NE * q + 2)
                        link(nc.vector.tensor_tensor(acc[:, :], acc[:, :], bank(5, 0, C), ALU.add))
                        link.end()
                        dve.sem_inc(ct_used, 1)
                    if attn and s in (1, 2):
                        turned_main(p, s - 1)
                    if attn and s == 3:
                        attended(p, 1 - par)
                    if attn and s == 5:
                        dve.wait_ge(xnT_done, p + 1)
                        nc.vector.tensor_copy(xnT[1 - par][:, :], bank(5, 0, P)).then_inc(xnT_ready, 1)
                    if attn and s == 6:
                        route(p)
                    if attn and s == 7:
                        weigh(p, 1 - par)
                    if moe and s == 7:
                        finish(q, par, isinstance(i, int) and q < 2)

            dve.wait_ge(cx_done, 1)
            nc.vector.tensor_tensor(cexp[:, :], bank(7, 0, C)[0:NE, :], c_("b2")[0:NE, :], ALU.add).then_inc(cx_ready, 1)
            step_main(1, 1, moe=False)
            step_main(2, 0)
            step_main(3, 1)
            with dve.Fori(2, NB // 2) as n:
                for par in range(2):
                    step_main(2 * n + par, par)
            step_main(NB, 0)
            step_main(NB + 1, 1, attn=False)


def _penalties():
    pen = np.full((3, ROWS, WD, ROWS + 2 * HALO, WD), BIG, np.float32)
    for kind, r0 in enumerate((0, ROWS, HT - ROWS)):
        for r in range(ROWS):
            top = min(max(r0 + r - HALO, 0), HT - KW_)
            for w in range(WD):
                left = min(max(w - HALO, 0), WD - KW_)
                at = top - (r0 - HALO)
                pen[kind, r, w, at:at + KW_, left:left + KW_] = 0.0
    return pen.reshape(3, P, WKEYS).transpose(1, 0, 2).reshape(P, 3 * WKEYS)


def _layouts(i):
    f = np.float32
    a = {k: np.asarray(v) for k, v in i.items()}
    rows = lambda v: np.broadcast_to(v.reshape(1, -1), (P, v.size))
    col = lambda v: v.reshape(-1, 1)
    qkv, qb = a["L0_conv_qkv_w"], a["L0_conv_qkv_b"]
    wvg = np.zeros((C, VG), f)
    wvg[:, :VW_COLS].reshape(C, NH, HP)[:, :, :HD] = qkv[:, 2 * C:].reshape(C, NH, HD)
    wvg[:, VW_COLS:] = a["L0_conv_g1_w"]
    bvg = np.zeros((VG,), f)
    bvg[:VW_COLS].reshape(NH, HP)[:, :HD] = qb[2 * C:].reshape(NH, HD)
    bvg[VW_COLS:] = a["L0_conv_g1_b"]
    proj = np.zeros((4, HP, 2, C), f)
    proj[:, :HD] = a["L0_conv_proj_w"].reshape(2, 4, HD, C).transpose(1, 2, 0, 3)
    wa = np.zeros((QPG, U, 2 * U), f)
    for g in range(QPG):
        wa[g, :, U - QPG + g] = a["L1_attn_Wa"][:, 0]
    b1 = a["L1_ffn_b1"].reshape(NE, FC, P).transpose(2, 0, 1)
    b1e = np.zeros((P, NE, FC, NE), f)
    for e in range(NE):
        b1e[:, e, :, e] = b1[:, e]
    b2 = np.zeros((P, C), f)
    b2[:NE] = a["L1_ffn_b2"]
    parts = {
        "wq": qkv[:, :C], "wk": qkv[:, C:2 * C], "wvg": wvg, "bvg": rows(bvg), "g2w": rows(a["L0_conv_g2_w"]),
        "proj": proj.reshape(P, 2 * C), "projb": rows(a["L0_conv_proj_b"]), "lng": rows(a["L0_conv_ln_g"]),
        "lnb": rows(a["L0_conv_ln_b"]), "wt": a["L1_attn_Wt"], "wx4": np.tile(a["L1_attn_Wx"], (1, QPG)),
        "wa": wa.reshape(P, 2 * U), "gate": a["L1_ffn_gate_w"], "gateb": rows(a["L1_ffn_gate_b"]),
        "b1": b1.reshape(P, NE * FC), "b1e": b1e.reshape(P, NE * FC * NE), "b2": b2, "bq": col(qb[:C]),
        "bk": col(qb[C:2 * C]), "g2b": rows(a["L0_conv_g2_b"]), "bh": col(np.tile(a["L1_attn_bh"], QPG)),
        "ba": rows(a["L1_attn_ba"]), "ident": np.eye(P, dtype=f), "tri": np.triu(np.ones((P, P), f)),
        "heads": (np.arange(P)[:, None] // HD == np.arange(NH)).astype(f),
        "first": rows(np.arange(NE, 0, -1).astype(f)), "pen": _penalties(),
    }
    cst = np.concatenate([np.ascontiguousarray(parts[n], dtype=f) for n, _ in _COLS], axis=1)
    rpb = a["L0_conv_rpb"]
    table = np.zeros((ROWS, WD, NH, ROWS + 2 * HALO, WD), f)
    for r in range(ROWS):
        for w in range(WD):
            lo, hi = max(0, w - KW_ + 1), min(WD, w + KW_)
            table[r, w, :, :, lo:hi] = rpb[:, HALO - r:HALO - r + ROWS + 2 * HALO, lo - w + KW_ - 1:hi - w + KW_ - 1]
    x = a["x"].reshape(NT, C)
    return {
        "cst": cst, "xT": np.ascontiguousarray(x.T), "x": np.ascontiguousarray(x),
        "bias": table.reshape(P, NH * WKEYS),
        "w1": np.ascontiguousarray(a["L1_ffn_w1"].transpose(1, 0, 2)).reshape(C, NE * FF),
        "w2": np.ascontiguousarray(a["L1_ffn_w2"].reshape(NE, FC, P, C).transpose(2, 0, 1, 3)).reshape(P, NE * FC * C),
    }


def kernel(**inputs):
    import concourse.bacc as bacc
    from concourse.bass_utils import run_bass_kernel_spmd

    arrays = {f"in_{k}": v for k, v in _layouts(inputs).items()}
    nc = bacc.Bacc("TRN2", target_bir_lowering=False, num_devices=1)
    args = [nc.dram_tensor(n, v.shape, mybir.dt.from_np(v.dtype), kind="ExternalInput").ap() for n, v in arrays.items()]
    out = nc.dram_tensor("out", (NT, C), F32, kind="ExternalOutput").ap()
    program(nc, *args, out)
    r = run_bass_kernel_spmd(nc, [arrays], core_ids=[0])
    return r.results[0]["out"].reshape(B, HT, WD, C)
```

```python
from contextlib import ExitStack

import numpy as np

import concourse.bass as bass
from concourse import mybir

F32 = mybir.dt.float32
BF16 = mybir.dt.bfloat16
I32 = mybir.dt.int32
U32 = mybir.dt.uint32
ALU = mybir.AluOpType
ACT = mybir.ActivationFunctionType
AX = mybir.AxisListType.X

P = 128
B, HT, WD, C = 2, 32, 32, 128
NT = B * HT * WD
L = HT * WD
ROWS = P // WD
NB = NT // P
BPI = NB // B
SLOTS = BPI + 2
KW_ = 7
HALO = KW_ // 2
NH, HD = 8, 16
WKEYS = (ROWS + 2 * HALO) * WD
WOFF = (ROWS - HALO) * WD
HP = 32
VW_COLS = NH * HP
U = 32
GH = C // 4
VG = VW_COLS + GH
QPG = P // U
CH = 8
NE, FF = 8, 512
FC = FF // P
CAP = -(-5 * NT // (4 * NE))
BIG = 1e30
FLT_MAX = float(np.finfo(np.float32).max)
SCALE = float(HD) ** -0.5

_COLS = [("wq", C), ("wk", C), ("wvg", VG), ("bvg", VG), ("g2w", GH), ("proj", 2 * C), ("projb", C),
         ("lng", C), ("lnb", C), ("wt", U), ("wx4", P), ("wa", 2 * U), ("gate", NE), ("gateb", NE),
         ("b1", NE * FC), ("b1e", NE * FC * NE), ("b2", C), ("bq", 1), ("bk", 1), ("g2b", 1),
         ("bh", 1), ("ba", 1), ("ident", P), ("tri", P), ("heads", NH), ("first", NE),
         ("pen", 3 * WKEYS)]
CST, _n = {}, 0
for _name, _w in _COLS:
    CST[_name] = (_n, _n + _w)
    _n += _w
CST_COLS = _n


class Chain:

    def __init__(self, eng, sem):
        self.eng, self.sem, self.n = eng, sem, 0

    def __call__(self, instruction):
        self.n += 1
        instruction.then_inc(self.sem, 1)
        self.eng.wait_ge(self.sem, self.n)

    def end(self):
        self.eng.sem_clear(self.sem)
        self.n = 0


def rsqrt_seed(nc, link, y, v, w):
    link(nc.vector.tensor_scalar(w.bitcast(I32), v.bitcast(I32), 1, None, ALU.arith_shift_right))
    link(nc.vector.tensor_scalar(y.bitcast(I32), w.bitcast(I32), -1.0, float(0x5F3759DF), ALU.mult, ALU.add))


def rsqrt_turn(nc, link, y, v, w):
    link(nc.vector.tensor_tensor(w, y, y, ALU.mult))
    link(nc.vector.tensor_tensor(w, w, v, ALU.mult))
    link(nc.vector.tensor_scalar(w, w, -0.5, 1.5, ALU.mult, ALU.add))
    link(nc.vector.tensor_tensor(y, y, w, ALU.mult))


def program(nc, cst_d, xT_d, x_d, bias_d, w1_d, w2_d, out_d):
    with ExitStack() as ctx:
        def sb(name, shape, dt=F32):
            return ctx.enter_context(nc.sbuf_tensor(name, shape, dt))

        def sem(name):
            return ctx.enter_context(nc.semaphore(name))

        cst = sb("cst", [P, CST_COLS])

        def c_(name, lo=0, hi=None):
            a, b = CST[name]
            return cst[:, a + lo:(a + hi if hi is not None else b)]

        tokens = sb("tokens", [P, 4, L])
        xT = tokens[:, 0:2, :].rearrange("p a t -> p (a t)")
        x_all = sb("x_all", [P, NB, C])
        y_all = sb("y_all", [P, NB, C])
        kT = sb("kT", [P, B * SLOTS * P])
        qT = tokens[:, 2:4, :].rearrange("p a t -> p (a t)")
        vg = sb("vg", [P, B * SLOTS, VG])
        gate = sb("gate", [P, NB])
        arena = sb("arena", [P, 4 * 4096])
        PW = 3 * P
        prob = [arena[:, i * NH * PW:(i + 1) * NH * PW].rearrange("p (h k) -> p h k", h=NH) for i in range(2)]
        o = 2 * NH * PW
        nlog = arena[:, o:o + NH * WKEYS].rearrange("p (h k) -> p h k", h=NH)
        o += NH * WKEYS
        btab = [arena[:, o + i * NH * WKEYS:o + (i + 1) * NH * WKEYS].rearrange("p (h k) -> p h k", h=NH)
                for i in range(3)]
        w1 = arena[:, 0:NE * FF].rearrange("p (e f) -> p e f", e=NE)
        w2 = arena[:, NE * FF:2 * NE * FF].rearrange("p (e c d) -> p e c d", e=NE, c=FC)
        o = 2 * NE * FF
        hid_ring = [arena[:, o + i * QPG * L:o + (i + 1) * QPG * L].rearrange("p (c j) -> p c j", c=QPG)
                    for i in range(2)]

        qw = [sb(f"qw{i}", [P, P]) for i in range(2)]
        kw = [sb(f"kw{i}", [P, WKEYS]) for i in range(2)]
        vw = [sb(f"vw{i}", [P, 3, VW_COLS]) for i in range(2)]
        early = sb("early", [P, 2 * NH * P])
        qm = [early[:, i * NH * P:(i + 1) * NH * P].rearrange("p (h q) -> p h q", h=NH) for i in range(2)]
        pts = [sb(f"pts{i}", [P, PW]) for i in range(2)]
        ots = sb("ots", [P, 2 * P])
        mn = [sb(f"mn{i}", [P, NH]) for i in range(2)]
        zs = [sb(f"zs{i}", [P, NH]) for i in range(2)]
        rz = [sb(f"rz{i}", [P, NH]) for i in range(2)]
        ytmp = sb("ytmp", [P, C])
        nbq = sb("nbq", [P, 1])
        hg2b = sb("hg2b", [P, 1])
        gz = sb("gz", [P, NB])
        gt = sb("gt", [P, NB])

        kcur = [sb(f"kcur{i}", [P, L]) for i in range(2)]
        xcur = [sb(f"xcur{i}", [P, BPI * C]) for i in range(2)]
        qcur = [sb(f"qcur{i}", [P, U]) for i in range(2)]
        kq_sum = [early[:, :].rearrange("p (c j) -> p c j", c=2), tokens[:, 0:4:3, :]]
        nwa = sb("nwa", [P, 2 * U])
        trib = sb("trib", [P, P], BF16)
        oneb = sb("oneb", [P, P], BF16)
        nb1 = sb("nb1", [P, NE * FC])
        cexp = sb("cexp", [NE, C])
        pm = sb("pm", [P, L])
        ptm = sb("ptm", [P, BPI, P])
        nmin = sb("nmin", [P, 1])
        zm = sb("zm", [P, 1])
        rzm = sb("rzm", [P, 1])
        t2 = [sb(f"t2_{i}", [P, C]) for i in range(2)]
        xn = sb("xn", [P, C])
        xnT = [sb(f"xnT{i}", [P, P]) for i in range(2)]
        stats = sb("stats", [P, 6])
        mv = sb("mv", [P, 2])
        sv = sb("sv", [P, NB])
        sy = sb("sy", [P, NB])
        sw = sb("sw", [P, NB])
        mean = sb("mean", [P, NB])
        lg = sb("lg", [P, NE])
        mx = sb("mx", [P, 1])
        nmx = sb("nmx", [P, 1])
        lge = sb("lge", [P, NE])
        zg = sb("zg", [P, 1])
        prb = sb("prb", [P, 1])
        oha = sb("oha", [P, NE])
        ohw = sb("ohw", [P, 1])
        oh = sb("oh", [P, NE])
        ohb = sb("ohb", [P, NE], BF16)
        osum = sb("osum", [P, NE], BF16)
        keep = sb("keep", [P, NE])
        msk = [sb(f"msk{i}", [P, NE]) for i in range(2)]
        mT = sb("mT", [NE, P])
        hids = [sb(f"hids{i}", [P, FC, P]) for i in range(2)]
        accs = [sb(f"acc{i}", [P, C]) for i in range(2)]
        bad = sb("bad", [P, 3, C], U32)
        fill = sb("fill", [P, 3, C])
        outs = [sb(f"outs{i}", [P, C]) for i in range(2)]

        ps = ctx.enter_context(nc.psum_tensor("ps", [P, 8 * 512], F32))

        def bank(i, lo=0, hi=512):
            return ps[:, 512 * i + lo:512 * i + hi]

        ld_cst, ld_x, ld_w = sem("ld_cst"), sem("ld_x"), sem("ld_w")
        ld_xT = [sem(f"ld_xT{i}") for i in range(4)]
        ld_bias = [sem(f"ld_bias{i}") for i in range(3)]
        small_ready, pads_ready, margins_ready = sem("small_ready"), sem("pads_ready"), sem("margins_ready")
        top_ready = sem("top_ready")
        q_done, k_done, v_done = sem("q_done"), sem("k_done"), sem("v_done")
        q_ready, k_ready, v_ready = sem("q_ready"), sem("k_ready"), sem("v_ready")
        gz_ready, gt_ready = sem("gz_ready"), sem("gt_ready")
        qk_ld = [sem(f"qk_ld{i}") for i in range(2)]
        v_ld = [sem(f"v_ld{i}") for i in range(2)]
        qm_ready, s_done, n_ready, p_ready = sem("qm_ready"), sem("s_done"), sem("n_ready"), sem("p_ready")
        rz_ready, pn_ready, pt_done = sem("rz_ready"), sem("pn_ready"), sem("pt_done")
        ptd_ready, pta_ready, pv_done = sem("ptd_ready"), sem("pta_ready"), sem("pv_done")
        ots_ready, proj_done, y_ready = sem("ots_ready"), sem("proj_done"), sem("y_ready")
        t_ready, tT_done, tT_ready = sem("t_ready"), sem("tT_done"), sem("tT_ready")
        k4_done, k4_ready, q4_done, q4_ready = sem("k4_done"), sem("k4_ready"), sem("q4_done"), sem("q4_ready")
        kq_ld = [sem(f"kq_ld{i}") for i in range(2)]
        xc_ld = [sem(f"xc_ld{i}") for i in range(2)]
        sum_ready, h_ready, h_used = sem("sum_ready"), sem("h_ready"), sem("h_used")
        nmin_ready, pm_ready = sem("nmin_ready"), sem("pm_ready")
        mt_done, mt_ready, pvm_done = sem("mt_done"), sem("mt_ready"), sem("pvm_done")
        xn_ready, xnT_done, xnT_ready = sem("xn_ready"), sem("xnT_done"), sem("xnT_ready")
        lg_done, mx_ready, ge_ready, oh_ready = sem("lg_done"), sem("mx_ready"), sem("ge_ready"), sem("oh_ready")
        cum_done, mask_ready = sem("cum_done"), sem("mask_ready")
        mT_done, mT_ready, ct_done, ct_used = sem("mT_done"), sem("mT_ready"), sem("ct_done"), sem("ct_used")
        hid_done, hid_ready, out_done, out_used = sem("hid_done"), sem("hid_ready"), sem("out_done"), sem("out_used")
        cx_done, cx_ready = sem("cx_done"), sem("cx_ready")
        fin_ready = sem("fin_ready")
        out_st = [sem(f"out_st{i}") for i in range(2)]
        dve_chain = sem("dve_chain")
        passed_dve, passed_pool = sem("passed_dve"), sem("passed_pool")

        def bias_table(engine, kind):
            pen = c_("pen", kind * WKEYS, (kind + 1) * WKEYS)[:, None, :].broadcast_to([P, NH, WKEYS])
            return engine.tensor_tensor(btab[kind], pen, btab[kind], ALU.subtract)

        block = ctx.enter_context(nc.Block())

        @block.sync
        def _(sp):
            pen = CST["pen"][0]
            sp.dma_start(cst[:, 0:pen], cst_d[:, 0:pen]).then_inc(ld_cst, 16)
            for i in range(4):
                sp.dma_start(xT[:, i * 512:(i + 1) * 512], xT_d[:, i * 512:(i + 1) * 512]).then_inc(ld_xT[i], 16)
            for i in range(3):
                sp.dma_start(cst[:, pen + i * WKEYS:pen + (i + 1) * WKEYS],
                             cst_d[:, pen + i * WKEYS:pen + (i + 1) * WKEYS]).then_inc(ld_bias[i], 16)
                sp.dma_start(btab[i].rearrange("p h k -> p (h k)"), bias_d).then_inc(ld_bias[i], 16)
                if i == 0:
                    sp.dma_start(x_all[:, :, :], x_d.rearrange("(n p) c -> p n c", p=P)).then_inc(ld_x, 16)
            sp.wait_ge(pads_ready, 2)
            for j in range(NB):
                par, slot = j % 2, j + 2 * (j // BPI)
                if j >= 2:
                    sp.wait_ge(s_done, NH * (j - 1))
                sp.wait_ge(q_ready, min(4, 1 + (j + 1) // 4))
                sp.wait_ge(k_ready, min(4, 1 + (j + 1) // 4))
                sp.dma_start(qw[par][:, :], qT[:, j * P:(j + 1) * P]).then_inc(qk_ld[par], 16)
                sp.dma_start(kw[par][:, :], kT[:, slot * P + WOFF:slot * P + WOFF + WKEYS]).then_inc(qk_ld[par], 16)
                if j >= 2:
                    sp.wait_ge(pv_done, NH * (j - 1))
                sp.wait_ge(v_ready, min(NB, j + 2))
                sp.dma_start(vw[par][:, :, :], vg[:, slot:slot + 3, 0:VW_COLS]).then_inc(v_ld[par], 16)
            sp.wait_ge(t_ready, 1)
            sp.wait_ge(k4_ready, 2)
            sp.wait_ge(q4_ready, 1)

            def stage(i, par, img):
                sp.dma_start(kcur[par][:, :], kT[:, img * L:(img + 1) * L]).then_inc(kq_ld[par], 16)
                sp.dma_start(qcur[par][:, :], qT[:, bass.ds(i * U, U)]).then_inc(kq_ld[par], 16)
                src = x_all[:, img * BPI:(img + 1) * BPI, :].rearrange("p n c -> p (n c)")
                sp.dma_start(xcur[par][:, :], src).then_inc(xc_ld[par], 16)

            def store(i, par):
                sp.wait_ge(fin_ready, i + 1)
                sp.dma_start(out_d[bass.ds(i * P, P), :], outs[par][:, :]).then_inc(out_st[par], 16)

            def turn(i, par, img, stores=True):
                sp.wait_ge(h_ready, CH * (i - 1))
                sp.wait_ge(pvm_done, i - 1)
                stage(i, par, img)
                if stores:
                    store(i - 3, 1 - par)

            stage(0, 0, 0)
            stage(1, 1, 0)
            sp.wait_ge(pt_done, NH * NB)
            sp.wait_ge(p_ready, NH * NB)
            sp.dma_start(w1, w1_d.rearrange("p (e f) -> p e f", e=NE)).then_inc(ld_w, 16)
            sp.dma_start(w2, w2_d.rearrange("p (e c d) -> p e c d", e=NE, c=FC)).then_inc(ld_w, 16)
            turn(2, 0, 0, stores=False)
            for i in (3, 4, 5, 6, 7):
                turn(i, i % 2, 0)
            sp.wait_ge(t_ready, 2)
            sp.wait_ge(k4_ready, 4)
            sp.wait_ge(q4_ready, 2)
            with sp.Fori(BPI // 2, NB // 2) as n:
                for par in range(2):
                    turn(2 * n + par, par, 1)
            for i in range(NB - 3, NB):
                store(i, i % 2)
            sp.wait_ge(out_st[0], 16 * NB // 2)
            sp.wait_ge(out_st[1], 16 * NB // 2)

        @block.gpsimd
        def _(pool):
            for b in range(B):
                for s in (0, SLOTS - 1):
                    at = b * SLOTS + s
                    nc.gpsimd.memset(kT[:, at * P:(at + 1) * P], 0.0)
                    last = nc.gpsimd.memset(vg[:, at, :], 0.0)
                last.then_inc(pads_ready, 1)
            for t in prob:
                nc.gpsimd.memset(t[:, :, 0:WOFF], 0.0)
                last = nc.gpsimd.memset(t[:, :, WOFF + WKEYS:PW], 0.0)
            last.then_inc(margins_ready, 1)

            def mask_heads(j, par, first=False):
                if not first:
                    pool.wait_ge(s_done, NH * (j - 1))
                pool.wait_ge(qk_ld[par], 16 * (j - par + 2))
                nc.gpsimd.tensor_tensor(qm[par], qw[par][:, None, :].broadcast_to([P, NH, P]),
                                        c_("heads")[:, :, None].broadcast_to([P, NH, P]),
                                        ALU.mult).then_inc(qm_ready, 1)

            def normalise(j, par, h0, h1):
                pool.wait_ge(rz_ready, 2 * j + h1 // 4)
                pool.sem_inc(passed_pool, 1)
                for h in range(h0, h1):
                    nc.gpsimd.tensor_scalar(prob[par][:, h, WOFF:WOFF + WKEYS], prob[par][:, h, WOFF:WOFF + WKEYS],
                                            rz[par][:, h:h + 1], 1.0, ALU.mult, ALU.mult).then_inc(pn_ready, 1)

            def step(j, par, more=True):
                normalise(j - 1, 1 - par, 4, NH)
                if more:
                    mask_heads(j + 1, 1 - par)
                if j is not NB:
                    normalise(j, par, 0, 4)

            pool.wait_ge(ld_cst, 16)
            pool.wait_ge(ld_bias[0], 32)
            bias_table(nc.gpsimd, 0).then_inc(top_ready, 1)
            mask_heads(0, 0, first=True)
            mask_heads(1, 1, first=True)
            normalise(0, 0, 0, 4)
            step(1, 1)
            with pool.Fori(1, NB // 2 - 1) as n:
                for par in range(2):
                    step(2 * n + par, par)
            step(NB - 2, 0)
            step(NB - 1, 1, more=False)
            step(NB, 0, more=False)

            def key_query_sums(i, par, s):
                keys, queries = kcur[par], qcur[par]
                if isinstance(i, int) and i == 0:
                    keys, queries = kT[:, 0:L], qT[:, 0:U]
                    if s == 0:
                        pool.wait_ge(s_done, NH * NB)
                        pool.wait_ge(k4_ready, 2)
                        pool.wait_ge(q4_ready, 1)
                elif s == 0:
                    pool.wait_ge(kq_ld[par], 16 * (i - par + 2))
                if s >= 2 or not (isinstance(i, int) and i == 0):
                    pool.wait_ge(h_ready, CH * i + s - 1)
                pool.sem_inc(passed_pool, 1)
                for c in range(2):
                    m = (2 + c) * CH + s
                    last = nc.gpsimd.tensor_scalar(kq_sum[s % 2][:, c, :], keys[:, :], queries[:, m:m + 1], 1.0,
                                                   ALU.add, ALU.mult)
                last.then_inc(sum_ready, 1)

            for i in range(2):
                for s in range(CH):
                    key_query_sums(i, i, s)
            with pool.Fori(1, NB // 2) as n:
                for par in range(2):
                    for s in range(CH):
                        key_query_sums(2 * n + par, par, s)

        @block.tensor
        def _(pe):
            pe.wait_ge(ld_cst, 16)
            for i in range(4):
                pe.wait_ge(ld_xT[i], 16)
                if i >= 2:
                    pe.wait_ge(q_ready, i - 1)
                nc.tensor.matmul(bank(i % 2), c_("wq"), xT[:, i * 512:(i + 1) * 512],
                                 start=True, stop=True).then_inc(q_done, 1)
                if i >= 2:
                    pe.wait_ge(k_ready, i - 1)
                nc.tensor.matmul(bank(2 + i % 2), c_("wk"), xT[:, i * 512:(i + 1) * 512],
                                 start=True, stop=True).then_inc(k_done, 1)
            for i in range(NB):
                if i >= 4:
                    pe.wait_ge(v_ready, i - 3)
                nc.tensor.matmul(bank(4 + i % 4, 0, VG), xT[:, i * P:(i + 1) * P], c_("wvg"),
                                 start=True, stop=True).then_inc(v_done, 1)
            pe.wait_ge(q_ready, 4)
            pe.wait_ge(k_ready, 4)
            pe.wait_ge(v_ready, NB)

            def scores(j, par, h):
                if h == 0:
                    pe.wait_ge(qm_ready, j + 1)
                    pe.wait_ge(qk_ld[par], 16 * (j - par + 2))
                if h >= 4 or not (isinstance(j, int) and j == 0):
                    pe.wait_ge(n_ready, NH * j + h - 3)
                nc.tensor.matmul(bank(h % 4, 0, WKEYS), qm[par][:, h, :], kw[par][:, :],
                                 start=True, stop=True).then_inc(s_done, 1)

            def turn_probs(j, par, h):
                pe.wait_ge(pn_ready, NH * j + h + 1)
                if h >= 2 or not (isinstance(j, int) and j == 0):
                    pe.wait_ge(pta_ready if h % 2 else ptd_ready, NH // 2 * j + h // 2)
                for k in range(3):
                    last = nc.tensor.transpose(bank(4 + h % 2, k * P, (k + 1) * P),
                                               prob[par][:, h, k * P:(k + 1) * P], c_("ident"))
                last.then_inc(pt_done, 1)

            def values(j, par, h):
                if h == 0:
                    pe.wait_ge(v_ld[par], 8 * (j - par + 2))
                    if not (isinstance(j, int) and j == 0):
                        pe.wait_ge(ots_ready, j)
                pe.wait_ge(pta_ready if h % 2 else ptd_ready, NH // 2 * j + h // 2 + 1)
                g, half = h % 4, h // 4
                for k in range(3):
                    last = nc.tensor.matmul(bank(6, half * P, (half + 1) * P)[g * HP:(g + 1) * HP, :],
                                            vw[par][:, k, h * HP:(h + 1) * HP],
                                            pts[h % 2][:, k * P:(k + 1) * P], start=(k == 0), stop=(k == 2))
                last.then_inc(pv_done, 1)

            def project(j):
                pe.wait_ge(ots_ready, j + 1)
                if not (isinstance(j, int) and j == 0):
                    pe.wait_ge(y_ready, j)
                for half in range(2):
                    last = nc.tensor.matmul(bank(7, 0, C), ots[:, half * P:(half + 1) * P],
                                            c_("proj", half * C, (half + 1) * C), start=(half == 0), stop=(half == 1))
                last.then_inc(proj_done, 1)

            def step(j, par, score=True, value=True, proj=True):
                for i in range(-2, NH):
                    if value and 0 <= i < NH:
                        turn_probs(j - 1, 1 - par, i)
                    if score and i + 2 < NH:
                        scores(j, par, i + 2)
                    if proj and score and i == -2:
                        values(j - 2, par, NH - 1)
                    if proj and i == 0:
                        project(j - 2)
                    if value and i >= 1:
                        values(j - 1, 1 - par, i - 1)

            pe.wait_ge(margins_ready, 1)
            step(0, 0, value=False, proj=False)
            step(1, 1, proj=False)
            with pe.Fori(1, NB // 2) as n:
                for par in range(2):
                    step(2 * n + par, par)

            def turn_tokens(img, banks):
                pe.wait_ge(t_ready, img + 1)
                for i in range(2):
                    for k in range(4):
                        last = nc.tensor.transpose(bank(banks[i], k * P, (k + 1) * P),
                                                   x_all[:, BPI * img + 4 * i + k, :], c_("ident"))
                    last.then_inc(tT_done, 1)

            def keys_queries(img, banks, q_bank):
                for i in range(2):
                    at = img * L + i * 512
                    pe.wait_ge(tT_ready, 2 * img + i + 1)
                    nc.tensor.matmul(bank(banks[i]), c_("wx4"), xT[:, at:at + 512],
                                     start=True, stop=True).then_inc(k4_done, 1)
                by4 = xT[:, img * L:(img + 1) * L].rearrange("p (m g) -> p g m", g=QPG)
                for g in range(QPG):
                    last = nc.tensor.matmul(bank(q_bank, 0, L // QPG)[g * U:(g + 1) * U, :], c_("wt"), by4[:, g, :],
                                            start=True, stop=True)
                last.then_inc(q4_done, 1)

            values(NB - 2, 0, NH - 1)
            pe.wait_ge(n_ready, NH * NB)
            turn_tokens(0, (0, 1))
            keys_queries(0, (2, 3), 0)
            step(NB, 0, score=False)
            values(NB - 1, 1, NH - 1)
            project(NB - 1)
            pe.wait_ge(k4_ready, 2)
            pe.wait_ge(q4_ready, 1)

            def energies(i, par, s):
                pe.wait_ge(h_ready, CH * i + s + 1)
                if s == 0 and not (isinstance(i, int) and i < 2):
                    pe.wait_ge(pm_ready, i - 1)
                for half in range(2):
                    for c in range(4):
                        last = nc.tensor.matmul(bank(2 * par + half)[c * U:(c + 1) * U, :],
                                                nwa[:, U - QPG - QPG * s:2 * U - QPG - QPG * s],
                                                hid_ring[s % 2][:, c, half * 512:(half + 1) * 512],
                                                start=(s == 0), stop=(s == CH - 1))
                last.then_inc(h_used, 1)

            def turn_main(i, half):
                if half == 0:
                    pe.wait_ge(pm_ready, i + 1)
                if half or not (isinstance(i, int) and i == 0):
                    pe.wait_ge(mt_ready, 2 * i + half)
                for k in range(4):
                    last = nc.tensor.transpose(bank(4, k * P, (k + 1) * P),
                                               pm[:, (4 * half + k) * P:(4 * half + k + 1) * P], c_("ident"))
                last.then_inc(mt_done, 1)

            def attend(i, par, after_experts, half):
                if half == 0:
                    pe.wait_ge(mt_ready, 2 * i + 2)
                    pe.wait_ge(xc_ld[par], 8 * (i - par + 2))
                    if after_experts:
                        pe.wait_ge(ct_used, i)
                for k in range(BPI // 2 * half, BPI // 2 * (half + 1)):
                    last = nc.tensor.matmul(bank(5, 0, C), ptm[:, k, :], xcur[par][:, k * C:(k + 1) * C],
                                            start=(k == 0), stop=(k == BPI - 1))
                if half:
                    last.then_inc(pvm_done, 1)

            def hidden(i, par, e, ahead):
                if e == 0:
                    pe.wait_ge(xnT_ready, i + 1)
                if ahead and e:
                    if e >= 2:
                        pe.wait_ge(hid_ready, NE * i + e - 1)
                elif e or not (isinstance(i, int) and i == 0):
                    pe.wait_ge(hid_ready, NE * i + e)
                for c in range(FC):
                    last = nc.tensor.matmul(bank(0 if ahead and e % 2 else 6, c * P, (c + 1) * P), w1[:, e, c * P:(c + 1) * P], xnT[par][:, :],
                                            start=True, stop=True)
                last.then_inc(hid_done, 1)

            def expert(i, e, ahead):
                pe.wait_ge(hid_ready, NE * i + e + 1)
                if ahead and e:
                    if e >= 2:
                        pe.wait_ge(out_used, NE * i + e - 1)
                elif e or not (isinstance(i, int) and i == 0):
                    pe.wait_ge(out_used, NE * i + e)
                if e == 0:
                    pe.wait_ge(cx_ready, 1)
                for c in range(FC):
                    last = nc.tensor.matmul(bank(1 if ahead and e % 2 else 7, 0, C), hids[e % 2][:, c, :], w2[:, e, c, :],
                                            start=(c == 0), stop=(c == FC - 1))
                last.then_inc(out_done, 1)

            def expert_bias(e):
                for c in range(FC):
                    k = e * FC + c
                    last = nc.tensor.matmul(bank(7, 0, C)[0:NE, :], c_("b1e", k * NE, (k + 1) * NE), w2[:, e, c, :],
                                            start=(k == 0), stop=(k == NE * FC - 1))
                last.then_inc(cx_done, 1)

            def step_main(i, par, energy=True, attn=True, moe=True, bias=False):
                p, q = i - 1, i - 2
                ahead = not energy
                for s in range(CH):
                    if moe and s == 0:
                        pe.wait_ge(xnT_ready, q + 1)
                        nc.tensor.matmul(bank(5, 0, NE), xnT[par][:, :], c_("gate"),
                                         start=True, stop=True).then_inc(lg_done, 1)
                    if moe and s == 2:
                        pe.wait_ge(mask_ready, q + 1)
                        nc.tensor.transpose(bank(5, 0, P)[0:NE, :], msk[par][:, :], c_("ident")).then_inc(mT_done, 1)
                    if moe and s == 3:
                        pe.wait_ge(mT_ready, q + 1)
                        pe.wait_ge(cx_ready, 1)
                        nc.tensor.matmul(bank(5, 0, C), mT[:, :], cexp[:, :], start=True, stop=True).then_inc(ct_done, 1)
                    if attn and s in (2, 3):
                        turn_main(p, s - 2)
                    if attn and s in (4, 5):
                        attend(p, 1 - par, moe, s - 4)
                    if moe and not (ahead and s):
                        hidden(q, par, s, ahead)
                    if moe and s == 1:
                        pe.wait_ge(oh_ready, q + 1)
                        nc.tensor.matmul(bank(5, 0, NE), trib[:, :], ohb[:, :], start=True, stop=False)
                        nc.tensor.matmul(bank(5, 0, NE), oneb[:, :], osum[:, :], start=False, stop=True).then_inc(cum_done, 1)
                    if energy:
                        energies(i, par, s)
                    if attn and s == 7:
                        pe.wait_ge(xn_ready, p + 1)
                        nc.tensor.transpose(bank(5, 0, P), xn[:, :], c_("ident")).then_inc(xnT_done, 1)
                    if moe and ahead and s + 1 < NE:
                        hidden(q, par, s + 1, ahead)
                    if moe:
                        expert(q, s, ahead)
                    if bias:
                        expert_bias(s)

            for s in range(CH):
                energies(0, 0, s)
                if s == CH - 2:
                    pe.wait_ge(pta_ready, NH // 2 * NB)
                    pe.wait_ge(ots_ready, NB)
                    pe.wait_ge(y_ready, NB)
                    turn_tokens(1, (4, 5))
            keys_queries(1, (6, 7), 4)
            pe.wait_ge(k4_ready, 4)
            pe.wait_ge(q4_ready, 2)
            pe.wait_ge(ld_w, 32)
            step_main(1, 1, moe=False, bias=True)
            with pe.Fori(1, NB // 2) as n:
                for par in range(2):
                    step_main(2 * n + par, par)
            step_main(NB, 0, energy=False)
            step_main(NB + 1, 1, energy=False, attn=False)

        @block.scalar
        def _(act):
            act.wait_ge(small_ready, 1)
            for i in range(4):
                act.wait_ge(q_done, i + 1)
                nc.scalar.activation(qT[:, i * 512:(i + 1) * 512], bank(i % 2), ACT.Identity,
                                     bias=nbq[:, :], scale=-SCALE).then_inc(q_ready, 1)
            act.wait_ge(margins_ready, 1)

            def soften(j, par, h):
                act.wait_ge(n_ready, NH * j + h + 1)
                if h == 0 and not (isinstance(j, int) and j < 2):
                    act.wait_ge(pt_done, NH * (j - 1))
                nc.scalar.activation(prob[par][:, h, WOFF:WOFF + WKEYS], nlog[:, h, :], ACT.Exp,
                                     bias=mn[par][:, h:h + 1], scale=-1.0,
                                     accum_out=zs[par][:, h:h + 1]).then_inc(p_ready, 1)

            def turned(j, h):
                act.wait_ge(pt_done, NH * j + h + 1)
                if h >= 2 or not (isinstance(j, int) and j == 0):
                    act.wait_ge(pv_done, NH * j + h - 1)
                nc.scalar.activation(pts[1][:, :], bank(5, 0, PW), ACT.Copy).then_inc(pta_ready, 1)

            def heads_out(j):
                act.wait_ge(pv_done, NH * (j + 1))
                if not (isinstance(j, int) and j == 0):
                    act.wait_ge(proj_done, j)
                nc.scalar.activation(ots[:, :], bank(6, 0, 2 * P), ACT.Copy).then_inc(ots_ready, 1)

            def step(j, par, score=True, value=True):
                for i in range(NH + 1):
                    if value and i % 2 == 1:
                        turned(j - 1, i)
                    if score and i >= 1:
                        soften(j, par, i - 1)
                if value:
                    heads_out(j - 1)

            step(0, 0, value=False)
            act.wait_ge(gz_ready, 1)
            nc.scalar.activation(gt[:, :], gz[:, :], ACT.Tanh, bias=hg2b[:, :], scale=0.5).then_inc(gt_ready, 1)
            step(1, 1)
            with act.Fori(1, NB // 2) as n:
                for par in range(2):
                    step(2 * n + par, par)

            for i in range(2):
                act.wait_ge(tT_done, i + 1)
                nc.scalar.activation(xT[:, i * 512:(i + 1) * 512], bank(i), ACT.Copy).then_inc(tT_ready, 1)
            for i in range(2):
                act.wait_ge(k4_done, i + 1)
                nc.scalar.activation(kT[:, i * 512:(i + 1) * 512], bank(2 + i), ACT.Identity,
                                     bias=c_("bh")).then_inc(k4_ready, 1)

            def hidden_units(i, par, s):
                keys, queries = kcur[par], qcur[par]
                if isinstance(i, int) and i == 0:
                    keys, queries = kT[:, 0:L], qT[:, 0:U]
                    if s == 0:
                        act.wait_ge(k4_ready, 2)
                        act.wait_ge(q4_ready, 1)
                elif s == 0:
                    act.wait_ge(kq_ld[par], 16 * (i - par + 2))
                if s >= 2 or not (isinstance(i, int) and i == 0):
                    act.wait_ge(h_used, CH * i + s - 1)
                for c in range(2):
                    m = c * CH + s
                    nc.scalar.activation(hid_ring[s % 2][:, c, :], keys[:, :], ACT.Tanh, bias=queries[:, m:m + 1])
                act.wait_ge(sum_ready, CH * i + s + 1)
                nc.scalar.activation(hid_ring[s % 2][:, 2:4, :], kq_sum[s % 2][:, :, :], ACT.Tanh).then_inc(h_ready, 1)

            def soften_main(i, par):
                act.wait_ge(nmin_ready, i + 1)
                if not (isinstance(i, int) and i == 0):
                    act.wait_ge(mt_done, 2 * i)
                nc.scalar.activation(pm[:, :], ps[:, par * L:(par + 1) * L], ACT.Exp, bias=nmin[:, :], scale=-1.0,
                                     accum_out=zm[:, :]).then_inc(pm_ready, 1)

            def step_main(i, par, energy=True, attn=True, moe=True):
                for s in range(CH):
                    if energy:
                        hidden_units(i, par, s)
                    if attn and s == 1:
                        soften_main(i - 1, 1 - par)
                    if moe and s == 1:
                        act.wait_ge(mx_ready, i - 1)
                        nc.scalar.activation(lge[:, :], lg[:, :], ACT.Exp, bias=nmx[:, :],
                                             accum_out=zg[:, :]).then_inc(ge_ready, 1)

            step_main(0, 0, attn=False, moe=False)
            step_main(1, 1, moe=False)
            with act.Fori(1, NB // 2) as n:
                for par in range(2):
                    step_main(2 * n + par, par)
            step_main(NB, 0, energy=False)
            step_main(NB + 1, 1, energy=False, attn=False)

        @block.vector
        def _(dve):
            link = Chain(dve, dve_chain)
            dve.wait_ge(ld_cst, 16)
            nc.vector.tensor_scalar(hg2b[:, :], c_("g2b"), 0.5, None, ALU.mult)
            nc.vector.tensor_scalar(nwa[:, :], c_("wa"), -1.0, None, ALU.mult)
            nc.vector.tensor_copy(trib[:, :], c_("tri"))
            nc.vector.memset(oneb[:, :], 1.0)
            nc.vector.memset(osum[:, :], 0.0)
            nc.vector.tensor_scalar(nb1[:, :], c_("b1"), -1.0, None, ALU.mult)
            for i, v in enumerate((0.0, 1e4, -1e4)):
                nc.vector.memset(fill[:, i, :], v)
            nc.vector.tensor_scalar(nbq[:, :], c_("bq"), -SCALE, None, ALU.mult).then_inc(small_ready, 1)

            def key_rows(i):
                dve.wait_ge(k_done, i + 1)
                at = (i // 2) * SLOTS * P + P + (i % 2) * 512
                nc.vector.tensor_scalar(kT[:, at:at + 512], bank(2 + i % 2), c_("bk"), None, ALU.add).then_inc(k_ready, 1)

            for i in range(4):
                key_rows(i)
            for i in range(NB):
                dve.wait_ge(v_done, i + 1)
                nc.vector.tensor_tensor(vg[:, i + 1 + 2 * (i // BPI), :], bank(4 + i % 4, 0, VG), c_("bvg"),
                                        ALU.add).then_inc(v_ready, 1)

            def gate_sums():
                for b in range(B):
                    hid = vg[:, b * SLOTS + 1:b * SLOTS + 1 + BPI, VW_COLS:VG]
                    g2 = c_("g2w")[:, None, :].broadcast_to([P, BPI, GH])
                    link(nc.vector.scalar_tensor_tensor(hid, hid, 0.0, g2, ALU.max, ALU.mult))
                    link(nc.vector.tensor_reduce(gz[:, b * BPI:(b + 1) * BPI], hid, AX, ALU.add))
                link.end()
                dve.sem_inc(gz_ready, 1)

            def bias_scores(j, par, h, table):
                dve.wait_ge(s_done, NH * j + h + 1)
                if not (isinstance(j, int) and j == 0):
                    dve.wait_ge(p_ready, NH * (j - 1) + h + 1)
                dve.sem_inc(passed_dve, 1)
                nc.vector.tensor_tensor_reduce(out=nlog[:, h, :], in0=bank(h % 4, 0, WKEYS), in1=btab[table][:, h, :],
                                               scale=1.0, scalar=3e38, op0=ALU.add, op1=ALU.min,
                                               accum_out=mn[par][:, h:h + 1]).then_inc(n_ready, 1)

            def norms(j, par, half):
                dve.wait_ge(p_ready, NH * j + 4 * half + 4)
                nc.vector.reciprocal(rz[par][:, 4 * half:4 * half + 4],
                                     zs[par][:, 4 * half:4 * half + 4]).then_inc(rz_ready, 1)

            def turned(j, h):
                dve.wait_ge(pt_done, NH * j + h + 1)
                if h >= 2 or not (isinstance(j, int) and j == 0):
                    dve.wait_ge(pv_done, NH * j + h - 1)
                nc.vector.tensor_copy(pts[h % 2][:, :], bank(4 + h % 2, 0, PW)).then_inc(
                    pta_ready if h % 2 else ptd_ready, 1)

            def gated(j):
                dve.wait_ge(proj_done, j + 1)
                link(nc.vector.tensor_tensor(ytmp[:, :], bank(7, 0, C), c_("projb"), ALU.add))
                sq = lambda t: t[:, j, :] if isinstance(j, int) else t[:, bass.ds(j, 1), :].rearrange("p n c -> p (n c)")
                g = gate[:, j:j + 1] if isinstance(j, int) else gate[:, bass.ds(j, 1)]
                link(nc.vector.scalar_tensor_tensor(sq(y_all), ytmp[:, :], g, sq(x_all), ALU.mult, ALU.add))
                link.end()
                dve.sem_inc(y_ready, 1)

            row = lambda n: c_(n)[:, None, :].broadcast_to([P, BPI, C])
            wide = lambda t: t[:, 0:BPI, None].broadcast_to([P, BPI, C])
            scratch = xT[:, L:2 * L].rearrange("p (n c) -> p n c", n=BPI)
            PARTS = 16
            NORM_AT = (1, 3, 6)

            def norm_part(img, part):
                first = part < 9
                y3, x3 = (t[:, img * BPI:(img + 1) * BPI, :] for t in (y_all, x_all))
                src, dst = (y3, y3) if first else (y3, x3)
                m, v, y, w = (t[:, 0:BPI] for t in (mean, sv, sy, sw))
                k = part if first else part - 9
                if k == 0:
                    link(nc.vector.tensor_reduce(m, src, AX, ALU.add))
                    link(nc.vector.tensor_scalar(m, m, 1.0 / C, None, ALU.mult))
                elif k == 1:
                    link(nc.vector.tensor_tensor(dst, src, wide(mean), ALU.subtract))
                elif k == 2:
                    link(nc.vector.tensor_tensor(scratch, dst, dst, ALU.mult))
                elif k == 3:
                    link(nc.vector.tensor_reduce(v, scratch, AX, ALU.add))
                    link(nc.vector.tensor_scalar(v, v, 1.0 / C, 1e-5, ALU.mult, ALU.add))
                elif k == 4:
                    rsqrt_seed(nc, link, y, v, w)
                    rsqrt_turn(nc, link, y, v, w)
                elif k == 5:
                    rsqrt_turn(nc, link, y, v, w)
                    rsqrt_turn(nc, link, y, v, w)
                elif k == 6:
                    link(nc.vector.tensor_tensor(dst, dst, wide(sy), ALU.mult))
                elif k == 7:
                    link(nc.vector.tensor_tensor(dst, dst, row("lng"), ALU.mult))
                elif k == 8:
                    link(nc.vector.tensor_tensor(dst, dst, row("lnb"), ALU.add))
                link.end()
                if part == PARTS - 1:
                    dve.sem_inc(t_ready, 1)

            def step(j, par, table=None, score=True, value=True, proj=True, parts=()):
                for i in range(-2, NH):
                    if value and i >= 0 and (i % 2 == 0 or not score):
                        turned(j - 1, i)
                    if score and i + 2 < NH:
                        bias_scores(j, par, i + 2, table)
                    if value and score and i == -2:
                        norms(j - 1, 1 - par, 1)
                    if proj and i == 1:
                        gated(j - 2)
                    if score and i == 4:
                        norms(j, par, 0)
                    if i in NORM_AT and NORM_AT.index(i) < len(parts):
                        norm_part(0, parts[NORM_AT.index(i)])

            TOP, INNER, BOTTOM = range(3)
            dve.wait_ge(top_ready, 1)
            step(0, 0, TOP, value=False, proj=False)
            dve.wait_ge(ld_bias[INNER], 32)
            link(bias_table(nc.vector, INNER))
            gate_sums()
            step(1, 1, INNER, proj=False)
            dve.wait_ge(gt_ready, 1)
            link(nc.vector.tensor_scalar(gate[:, :], gt[:, :], 0.5, 0.5, ALU.mult, ALU.add))
            dve.wait_ge(ld_bias[BOTTOM], 32)
            link(bias_table(nc.vector, BOTTOM))
            link.end()
            dve.wait_ge(ld_x, 16)
            step(2, 0, INNER)
            with dve.Fori(0, 2) as n:
                for k in range(2):
                    step(2 * n + 3 + k, (3 + k) % 2, INNER)
            done = 0
            for j in range(BPI - 1, NB):
                kind = (INNER, TOP, BOTTOM)[(j % BPI == 0) + 2 * (j % BPI == BPI - 1)]
                count = min(len(NORM_AT), PARTS - done) if j > BPI else 0
                step(j, j % 2, kind, parts=range(done, done + count))
                done += count
            norms(NB - 1, 1, 1)
            dve.wait_ge(q4_done, 1)
            nc.vector.tensor_copy(qT[:, 0:L // QPG], bank(0, 0, L // QPG)).then_inc(q4_ready, 1)
            step(NB, 0, score=False)
            dve.wait_ge(pv_done, NH * NB)
            dve.wait_ge(proj_done, NB - 1)
            nc.vector.tensor_copy(ots[:, :], bank(6, 0, 2 * P)).then_inc(ots_ready, 1)
            gated(NB - 1)
            for part in range(PARTS):
                norm_part(1, part)
            for i in range(2):
                dve.wait_ge(tT_done, 3 + i)
                nc.vector.tensor_copy(xT[:, L + i * 512:L + (i + 1) * 512], bank(4 + i)).then_inc(tT_ready, 1)
            for i in range(2):
                dve.wait_ge(k4_done, 3 + i)
                nc.vector.tensor_scalar(kT[:, L + i * 512:L + (i + 1) * 512], bank(6 + i), c_("bh"), None,
                                        ALU.add).then_inc(k4_ready, 1)
            dve.wait_ge(q4_done, 2)
            nc.vector.tensor_copy(qT[:, L // QPG:2 * L // QPG], bank(4, 0, L // QPG)).then_inc(q4_ready, 1)

            def least(i, par):
                dve.wait_ge(h_used, CH * (i + 1))
                link(nc.vector.tensor_reduce(nmin[:, :], ps[:, par * L:(par + 1) * L], AX, ALU.min))
                nc.vector.tensor_scalar(nmin[:, :], nmin[:, :], c_("ba"), c_("ba"), ALU.subtract, ALU.add).then_inc(nmin_ready, 1)
                link.end()

            def turned_main(i, half):
                dve.wait_ge(mt_done, 2 * i + half + 1)
                if half == 0 and not (isinstance(i, int) and i == 0):
                    dve.wait_ge(pvm_done, i)
                nc.vector.tensor_copy(ptm[:, 4 * half:4 * half + 4, :].rearrange("p k q -> p (k q)"),
                                      bank(4)).then_inc(mt_ready, 1)

            def attended(i, par):
                dve.wait_ge(pvm_done, i + 1)
                link(nc.vector.reciprocal(rzm[:, :], zm[:, :]))
                t = y_all[:, i, :] if isinstance(i, int) else y_all[:, bass.ds(i, 1), :].rearrange("p n c -> p (n c)")
                link(nc.vector.scalar_tensor_tensor(t2[par][:, :], bank(5, 0, C), rzm[:, :], t, ALU.mult, ALU.add))
                link(nc.vector.bn_stats(stats[:, :], t2[par][:, :]))
                link(nc.vector.bn_aggr(mv[:, :], stats[:, :]))
                link(nc.vector.tensor_scalar(sv[:, 0:1], mv[:, 1:2], 1e-5, None, ALU.add))
                rsqrt_seed(nc, link, sy[:, 0:1], sv[:, 0:1], sw[:, 0:1])
                rsqrt_turn(nc, link, sy[:, 0:1], sv[:, 0:1], sw[:, 0:1])
                link.end()

            def normed(i, par):
                for _ in range(2):
                    rsqrt_turn(nc, link, sy[:, 0:1], sv[:, 0:1], sw[:, 0:1])
                nc.vector.tensor_scalar(xn[:, :], t2[par][:, :], mv[:, 0:1], sy[:, 0:1], ALU.subtract,
                                        ALU.mult).then_inc(xn_ready, 1)
                link.end()

            def route(i):
                dve.wait_ge(lg_done, i + 1)
                link(nc.vector.tensor_tensor(lg[:, :], bank(5, 0, NE), c_("gateb"), ALU.add))
                link(nc.vector.tensor_reduce(mx[:, :], lg[:, :], AX, ALU.max))
                nc.vector.tensor_scalar(nmx[:, :], mx[:, :], -1.0, None, ALU.mult).then_inc(mx_ready, 1)
                link(nc.vector.tensor_scalar(oha[:, :], lg[:, :], mx[:, :], None, ALU.is_equal))
                link(nc.vector.tensor_tensor(oha[:, :], oha[:, :], c_("first"), ALU.mult))
                link(nc.vector.tensor_reduce(ohw[:, :], oha[:, :], AX, ALU.max))
                link(nc.vector.tensor_scalar(oh[:, :], oha[:, :], ohw[:, :], None, ALU.is_equal))
                nc.vector.tensor_copy(ohb[:, :], oh[:, :]).then_inc(oh_ready, 1)
                link.end()

            def weigh(i, par):
                dve.wait_ge(cum_done, i + 1)
                dve.wait_ge(ge_ready, i + 1)
                link(nc.vector.reciprocal(prb[:, :], zg[:, :]))
                link(nc.vector.tensor_scalar(keep[:, :], bank(5, 0, NE), CAP + 0.5, prb[:, :], ALU.is_lt, ALU.mult))
                link(nc.vector.tensor_tensor(osum[:, :], osum[:, :], ohb[:, :], ALU.add))
                nc.vector.tensor_tensor(msk[par][:, :], keep[:, :], oh[:, :], ALU.mult).then_inc(mask_ready, 1)
                link.end()

            def hidden(i, e, ahead):
                dve.wait_ge(hid_done, NE * i + e + 1)
                if e >= 2 or not (isinstance(i, int) and i == 0):
                    dve.wait_ge(out_done, NE * i + e - 1)
                nc.vector.tensor_tensor(hids[e % 2][:, :, :], bank(0 if ahead and e % 2 else 6).rearrange("p (c t) -> p c t", c=FC),
                                        nb1[:, e * FC:(e + 1) * FC, None].broadcast_to([P, FC, P]),
                                        ALU.max).then_inc(hid_ready, 1)

            def combine(i, par, e, ahead=False):
                out, acc = bank(1 if ahead and e % 2 else 7, 0, C), accs[par]
                dve.wait_ge(out_done, NE * i + e + 1)
                w = msk[par][:, e:e + 1]
                if e == 0:
                    dve.wait_ge(mask_ready, i + 1)
                    if not (isinstance(i, int) and i < 2):
                        dve.wait_ge(fin_ready, i - 1)
                    nc.vector.tensor_scalar(acc[:, :], out, w, None, ALU.mult).then_inc(out_used, 1)
                else:
                    dve.wait_ge(out_used, NE * i + e)
                    if e == 3:
                        dve.wait_ge(ct_used, i + 1)
                    nc.vector.scalar_tensor_tensor(acc[:, :], out, w, acc[:, :], ALU.mult, ALU.add).then_inc(out_used, 1)

            def finish(i, par):
                acc = accs[par]
                dve.wait_ge(out_used, NE * (i + 1))
                if not (isinstance(i, int) and i < 2):
                    dve.wait_ge(out_st[par], 8 * (i - par))
                link(nc.vector.tensor_tensor(bad[:, 0, :], acc[:, :], acc[:, :], ALU.not_equal))
                link(nc.vector.tensor_scalar(bad[:, 1, :], acc[:, :], FLT_MAX, None, ALU.is_gt))
                link(nc.vector.tensor_scalar(bad[:, 2, :], acc[:, :], -FLT_MAX, None, ALU.is_lt))
                for k in range(3):
                    link(nc.vector.copy_predicated(acc[:, :], bad[:, k, :], fill[:, k, :]))
                nc.vector.tensor_tensor(outs[par][:, :], acc[:, :], t2[par][:, :], ALU.add).then_inc(fin_ready, 1)
                link.end()

            def step_main(i, par, attn=True, moe=True, last=True, ahead=False, after=False):
                p, q = i - 1, i - 2
                for s in range(CH):
                    if attn and ahead and s == 0:
                        least(p, 1 - par)
                    if last and s == 0:
                        combine(i - 3, 1 - par, NE - 1, after)
                    if attn and not ahead and s == 0:
                        least(p, 1 - par)
                    if moe and not ahead and s >= 2:
                        combine(q, par, s - 1)
                    if moe:
                        hidden(q, s, ahead)
                    if moe and s == 0:
                        route(q)
                    if moe and ahead and s >= 2:
                        combine(q, par, s - 1, ahead)
                    if moe and s == 1:
                        weigh(q, par)
                        combine(q, par, 0)
                    if moe and s == 2:
                        dve.wait_ge(mT_done, q + 1)
                        nc.vector.tensor_copy(mT[:, :], bank(5, 0, P)[0:NE, :]).then_inc(mT_ready, 1)
                    if moe and s == 3:
                        dve.wait_ge(ct_done, q + 1)
                        dve.wait_ge(out_used, NE * q + 3)
                        nc.vector.tensor_tensor(accs[par][:, :], accs[par][:, :], bank(5, 0, C),
                                                ALU.add).then_inc(ct_used, 1)
                    if attn and s in (2, 3):
                        turned_main(p, s - 2)
                    if last and s == (4 if moe else 0):
                        finish(i - 3, 1 - par)
                    if attn and s == 5:
                        attended(p, 1 - par)
                    if attn and s == (5 if ahead else 6):
                        normed(p, 1 - par)
                    if attn and s == 7:
                        dve.wait_ge(xnT_done, p + 1)
                        nc.vector.tensor_copy(xnT[1 - par][:, :], bank(5, 0, P)).then_inc(xnT_ready, 1)

            step_main(1, 1, moe=False, last=False)
            dve.wait_ge(cx_done, NE)
            nc.vector.tensor_tensor(cexp[:, :], bank(7, 0, C)[0:NE, :], c_("b2")[0:NE, :], ALU.add).then_inc(cx_ready, 1)
            step_main(2, 0, last=False)
            step_main(3, 1)
            with dve.Fori(2, NB // 2) as n:
                for par in range(2):
                    step_main(2 * n + par, par)
            step_main(NB, 0, ahead=True)
            step_main(NB + 1, 1, attn=False, ahead=True, after=True)
            step_main(NB + 2, 0, attn=False, moe=False, after=True)


def _penalties():
    pen = np.full((3, ROWS, WD, ROWS + 2 * HALO, WD), BIG, np.float32)
    for kind, r0 in enumerate((0, ROWS, HT - ROWS)):
        for r in range(ROWS):
            top = min(max(r0 + r - HALO, 0), HT - KW_)
            for w in range(WD):
                left = min(max(w - HALO, 0), WD - KW_)
                at = top - (r0 - HALO)
                pen[kind, r, w, at:at + KW_, left:left + KW_] = 0.0
    return pen.reshape(3, P, WKEYS).transpose(1, 0, 2).reshape(P, 3 * WKEYS)


def _layouts(i):
    f = np.float32
    a = {k: np.asarray(v) for k, v in i.items()}
    rows = lambda v: np.broadcast_to(v.reshape(1, -1), (P, v.size))
    col = lambda v: v.reshape(-1, 1)
    qkv, qb = a["L0_conv_qkv_w"], a["L0_conv_qkv_b"]
    wvg = np.zeros((C, VG), f)
    wvg[:, :VW_COLS].reshape(C, NH, HP)[:, :, :HD] = qkv[:, 2 * C:].reshape(C, NH, HD)
    wvg[:, VW_COLS:] = a["L0_conv_g1_w"]
    bvg = np.zeros((VG,), f)
    bvg[:VW_COLS].reshape(NH, HP)[:, :HD] = qb[2 * C:].reshape(NH, HD)
    bvg[VW_COLS:] = a["L0_conv_g1_b"]
    proj = np.zeros((4, HP, 2, C), f)
    proj[:, :HD] = a["L0_conv_proj_w"].reshape(2, 4, HD, C).transpose(1, 2, 0, 3)
    wa = np.zeros((QPG, U, 2 * U), f)
    for g in range(QPG):
        wa[g, :, U - QPG + g] = a["L1_attn_Wa"][:, 0]
    b1 = a["L1_ffn_b1"].reshape(NE, FC, P).transpose(2, 0, 1)
    b1e = np.zeros((P, NE, FC, NE), f)
    for e in range(NE):
        b1e[:, e, :, e] = b1[:, e]
    b2 = np.zeros((P, C), f)
    b2[:NE] = a["L1_ffn_b2"]
    parts = {
        "wq": qkv[:, :C], "wk": qkv[:, C:2 * C], "wvg": wvg, "bvg": rows(bvg), "g2w": rows(a["L0_conv_g2_w"]),
        "proj": proj.reshape(P, 2 * C), "projb": rows(a["L0_conv_proj_b"]), "lng": rows(a["L0_conv_ln_g"]),
        "lnb": rows(a["L0_conv_ln_b"]), "wt": a["L1_attn_Wt"], "wx4": np.tile(a["L1_attn_Wx"], (1, QPG)),
        "wa": wa.reshape(P, 2 * U), "gate": a["L1_ffn_gate_w"], "gateb": rows(a["L1_ffn_gate_b"]),
        "b1": b1.reshape(P, NE * FC), "b1e": b1e.reshape(P, NE * FC * NE), "b2": b2, "bq": col(qb[:C]),
        "bk": col(qb[C:2 * C]), "g2b": rows(a["L0_conv_g2_b"]), "bh": col(np.tile(a["L1_attn_bh"], QPG)),
        "ba": rows(a["L1_attn_ba"]), "ident": np.eye(P, dtype=f), "tri": np.triu(np.ones((P, P), f)),
        "heads": (np.arange(P)[:, None] // HD == np.arange(NH)).astype(f),
        "first": rows(np.arange(NE, 0, -1).astype(f)), "pen": _penalties(),
    }
    cst = np.concatenate([np.ascontiguousarray(parts[n], dtype=f) for n, _ in _COLS], axis=1)
    rpb = a["L0_conv_rpb"]
    table = np.zeros((ROWS, WD, NH, ROWS + 2 * HALO, WD), f)
    for r in range(ROWS):
        for w in range(WD):
            lo, hi = max(0, w - KW_ + 1), min(WD, w + KW_)
            table[r, w, :, :, lo:hi] = rpb[:, HALO - r:HALO - r + ROWS + 2 * HALO, lo - w + KW_ - 1:hi - w + KW_ - 1]
    x = a["x"].reshape(NT, C)
    return {
        "cst": cst, "xT": np.ascontiguousarray(x.T), "x": np.ascontiguousarray(x),
        "bias": table.reshape(P, NH * WKEYS),
        "w1": np.ascontiguousarray(a["L1_ffn_w1"].transpose(1, 0, 2)).reshape(C, NE * FF),
        "w2": np.ascontiguousarray(a["L1_ffn_w2"].reshape(NE, FC, P, C).transpose(2, 0, 1, 3)).reshape(P, NE * FC * C),
    }


def kernel(**inputs):
    import concourse.bacc as bacc
    from concourse.bass_utils import run_bass_kernel_spmd

    arrays = {f"in_{k}": v for k, v in _layouts(inputs).items()}
    nc = bacc.Bacc("TRN2", target_bir_lowering=False, num_devices=1)
    args = [nc.dram_tensor(n, v.shape, mybir.dt.from_np(v.dtype), kind="ExternalInput").ap() for n, v in arrays.items()]
    out = nc.dram_tensor("out", (NT, C), F32, kind="ExternalOutput").ap()
    program(nc, *args, out)
    r = run_bass_kernel_spmd(nc, [arrays], core_ids=[0])
    return r.results[0]["out"].reshape(B, HT, WD, C)
```
